# Optimizing a Trainium2 kernel written in Bass

```python
import numpy as np
import jax
import jax.numpy as jnp

def _softmax(x, axis=-1):
    return jax.nn.softmax(x, axis=axis)

def _gelu(x):
    return jax.nn.gelu(x, approximate=True)

def _silu(x):
    return jax.nn.silu(x)

def _sigmoid(x):
    return jax.nn.sigmoid(x)

def _layernorm(x, axis=-1, eps=1e-05):
    m = jnp.mean(x, axis=axis, keepdims=True)
    v = jnp.var(x, axis=axis, keepdims=True)
    return (x - m) / jnp.sqrt(v + eps)

def _scatter_add(tgt, idx, src, axis=0):
    return tgt.at[idx].add(src)

def _segment_sum(src, seg, n):
    return jax.ops.segment_sum(src, seg, n)
kernel_name = 'mk_gnn_preln_d4_gnn_r8_decbd7'

def setup_inputs(seed: int=0):
    np.random.seed(seed)
    _w = jnp.asarray

    def _rec_inputs():
        import jax
        import jax.numpy as jnp
        _gk = jax.random.key(seed)
        x = -0.000202 + 1 * jax.random.normal(jax.random.fold_in(_gk, 1), (12500, 64), jnp.float32)
        src = jax.random.randint(jax.random.fold_in(_gk, 2), (400000,), 0, 12500, jnp.int32)
        dst = jax.random.randint(jax.random.fold_in(_gk, 3), (400000,), 0, 12500, jnp.int32)
        _o = jnp.argsort(dst, stable=True)
        src = src[_o]
        dst = dst[_o]
        return (x, src, dst)
    x, src, dst = _rec_inputs()

    def _L0_gnn_setup():
        import jax, jax.numpy as jnp
        import numpy as np
        N_NODES = 12500
        NUM_LAYERS = 2
        key = jax.random.key(seed)
        k1, k2 = jax.random.split(key)
        x = jax.random.normal(k1, (N_NODES, 64), dtype=jnp.float32)
        edge_index = jax.random.randint(k2, (2, 400000), 0, N_NODES, dtype=jnp.int64)
        alpha = jnp.full((NUM_LAYERS + 1,), 1.0 / (NUM_LAYERS + 1), dtype=jnp.float32)
        return {'x': x, 'edge_index': edge_index, 'alpha': alpha}
    _L0_gnn_all = _L0_gnn_setup()
    _L0_gnn_in = {k: v for k, v in _L0_gnn_all.items() if k in ('alpha',)}
    del _L0_gnn_all

    def _L1_gnn_setup():
        import jax, jax.numpy as jnp
        import numpy as np
        N_NODES = 12500
        N_EDGES = 100000
        D = 64
        H = 4
        key = jax.random.key(seed)
        k1, k2, k3, k4, k5 = jax.random.split(key, 5)
        xavier = float(np.sqrt(2.0 / (D + D)))
        all_embeddings = jax.random.normal(k1, (N_NODES, D), dtype=jnp.float32)
        Wq = jax.random.normal(k2, (D, D), dtype=jnp.float32) * xavier
        Wk = jax.random.normal(k3, (D, D), dtype=jnp.float32) * xavier
        Wv = jax.random.normal(k4, (D, D), dtype=jnp.float32) * xavier
        edge_index = jax.random.randint(k5, (2, N_EDGES), 0, N_NODES, dtype=jnp.int32)
        return {'all_embeddings': all_embeddings, 'Wq': Wq, 'Wk': Wk, 'Wv': Wv, 'edge_index': edge_index}
    _L1_gnn_all = _L1_gnn_setup()
    _L1_gnn_in = {k: v for k, v in _L1_gnn_all.items() if k in ('Wq', 'Wk', 'Wv')}
    del _L1_gnn_all

    def _L2_gnn_setup():
        import jax, jax.numpy as jnp
        import numpy as np
        N_NODES = 12500
        N_EDGES = 200000
        D_FEAT = 64
        key = jax.random.key(seed)
        k1, k2 = jax.random.split(key)
        x = jax.random.normal(k1, (N_NODES, D_FEAT), dtype=jnp.float32)
        edge_index = jax.random.randint(k2, (2, N_EDGES), 0, N_NODES, dtype=jnp.int64)
        return {'x': x, 'edge_index': edge_index}
    _L2_gnn_all = _L2_gnn_setup()
    _L2_gnn_in = {k: v for k, v in _L2_gnn_all.items() if k in ()}
    del _L2_gnn_all

    def _L3_gnn_setup():
        import jax, jax.numpy as jnp
        import numpy as np
        NEG_SLOPE = 0.2

        def _gat_layer(x, src, dst, n_nodes, W, a_src, a_dst, b):
            h = x @ W
            alpha_s = h @ a_src
            alpha_d = h @ a_dst
            e = jax.nn.leaky_relu(alpha_s[src] + alpha_d[dst], NEG_SLOPE)
            m = jax.ops.segment_max(e, dst, num_segments=n_nodes)
            w = jnp.exp(e - m[dst])
            z = jax.ops.segment_sum(w, dst, num_segments=n_nodes)
            alpha = w / (z[dst] + 1e-16)
            out = jax.ops.segment_sum(alpha[:, None] * h[src], dst, num_segments=n_nodes)
            return out + b
        key = jax.random.key(seed)
        N, E, D_IN, D_H, D_OUT = (6250, 100000, 64, 64, 64)
        ks = jax.random.split(key, 12)
        x = jax.random.normal(ks[0], (N, D_IN), dtype=jnp.float32)
        edge_index = jax.random.randint(ks[1], (2, E), 0, N, dtype=jnp.int64)
        s = 1.0 / np.sqrt(D_IN)
        W1 = jax.random.normal(ks[2], (D_IN, D_H), dtype=jnp.float32) * s
        a_src1 = jax.random.normal(ks[3], (D_H,), dtype=jnp.float32) * s
        a_dst1 = jax.random.normal(ks[4], (D_H,), dtype=jnp.float32) * s
        b1 = jnp.zeros((D_H,), dtype=jnp.float32)
        s2 = 1.0 / np.sqrt(D_H)
        W2 = jax.random.normal(ks[5], (D_H, D_OUT), dtype=jnp.float32) * s2
        a_src2 = jax.random.normal(ks[6], (D_OUT,), dtype=jnp.float32) * s2
        a_dst2 = jax.random.normal(ks[7], (D_OUT,), dtype=jnp.float32) * s2
        b2 = jnp.zeros((D_OUT,), dtype=jnp.float32)
        return {'x': x, 'edge_index': edge_index, 'W1': W1, 'a_src1': a_src1, 'a_dst1': a_dst1, 'b1': b1, 'W2': W2, 'a_src2': a_src2, 'a_dst2': a_dst2, 'b2': b2}
    _L3_gnn_all = _L3_gnn_setup()
    _L3_gnn_in = {k: v for k, v in _L3_gnn_all.items() if k in ('W1', 'a_src1', 'a_dst1', 'b1', 'W2', 'a_src2', 'a_dst2', 'b2')}
    del _L3_gnn_all
    return {'x': x, 'src': src, 'dst': dst, 'L0_gnn_alpha': _L0_gnn_in['alpha'], 'L1_gnn_Wq': _L1_gnn_in['Wq'], 'L1_gnn_Wk': _L1_gnn_in['Wk'], 'L1_gnn_Wv': _L1_gnn_in['Wv'], 'L3_gnn_W1': _L3_gnn_in['W1'], 'L3_gnn_a_src1': _L3_gnn_in['a_src1'], 'L3_gnn_a_dst1': _L3_gnn_in['a_dst1'], 'L3_gnn_b1': _L3_gnn_in['b1'], 'L3_gnn_W2': _L3_gnn_in['W2'], 'L3_gnn_a_src2': _L3_gnn_in['a_src2'], 'L3_gnn_a_dst2': _L3_gnn_in['a_dst2'], 'L3_gnn_b2': _L3_gnn_in['b2']}

def reference(x, src, dst, L0_gnn_alpha, L1_gnn_Wq, L1_gnn_Wk, L1_gnn_Wv, L3_gnn_W1, L3_gnn_a_src1, L3_gnn_a_dst1, L3_gnn_b1, L3_gnn_W2, L3_gnn_a_src2, L3_gnn_a_dst2, L3_gnn_b2):
    import jax
    import jax.numpy as jnp

    def _L0_gnn_ref(x, edge_index, alpha):
        import jax, jax.numpy as jnp
        import numpy as np
        N_NODES = 12500
        NUM_LAYERS = 2
        row, col = (edge_index[0], edge_index[1])
        n = x.shape[0]
        ew = jnp.ones(row.shape[0], dtype=x.dtype)
        deg = jax.ops.segment_sum(ew, col, num_segments=n)
        dis = jnp.where(deg > 0, jax.lax.rsqrt(jnp.maximum(deg, 1.0)), 0.0).astype(x.dtype)
        norm = dis[row] * ew * dis[col]
        out = x * alpha[0]
        for i in range(NUM_LAYERS):
            msg = x[row] * norm[:, None]
            x = jax.ops.segment_sum(msg, col, num_segments=n)
            out = out + x * alpha[i + 1]
        return out

    def _L1_gnn_ref(all_embeddings, Wq, Wk, Wv, edge_index):
        import jax, jax.numpy as jnp
        import numpy as np
        N_NODES = 12500
        N_EDGES = 100000
        D = 64
        H = 4
        rows, cols = (edge_index[0], edge_index[1])
        n_nodes = all_embeddings.shape[0]
        e = rows.shape[0]
        dh = D // H
        row_emb = all_embeddings[rows]
        col_emb = all_embeddings[cols]
        q = (row_emb @ Wq).reshape(e, H, dh)
        k = (col_emb @ Wk).reshape(e, H, dh)
        v = (col_emb @ Wv).reshape(e, H, dh)
        att = jnp.einsum('ehd,ehd->eh', q, k)
        att = jnp.clip(att, -10.0, 10.0)
        exp_att = jnp.exp(att)
        att_norm = jax.ops.segment_sum(exp_att, rows, num_segments=n_nodes)
        att = exp_att / (att_norm[rows] + 1e-08)
        out_e = (att[:, :, None] * v).reshape(e, D)
        out = jax.ops.segment_sum(out_e, rows, num_segments=n_nodes)
        return out

    def _L2_gnn_ref(x, edge_index):
        import jax, jax.numpy as jnp
        import numpy as np
        N_NODES = 12500
        N_EDGES = 200000
        D_FEAT = 64
        row, col = (edge_index[0], edge_index[1])
        n = x.shape[0]
        deg = jax.ops.segment_sum(jnp.ones(row.shape[0], dtype=x.dtype), row, num_segments=n)
        deg_inv_sqrt = jnp.where(deg > 0, jax.lax.rsqrt(jnp.maximum(deg, 1.0)) * jnp.where(deg > 0, 1.0, 0.0), 0.0)
        deg_inv_sqrt = jnp.where(deg > 0, jax.lax.rsqrt(jnp.maximum(deg, 1.0)), 0.0)
        norm = deg_inv_sqrt[row] * deg_inv_sqrt[col]
        msgs = x[col] * norm[:, None]
        out = jax.ops.segment_sum(msgs, row, num_segments=n)
        return out

    def _L3_gnn_ref(x, edge_index, W1, a_src1, a_dst1, b1, W2, a_src2, a_dst2, b2):
        import jax, jax.numpy as jnp
        import numpy as np
        NEG_SLOPE = 0.2

        def _gat_layer(x, src, dst, n_nodes, W, a_src, a_dst, b):
            h = x @ W
            alpha_s = h @ a_src
            alpha_d = h @ a_dst
            e = jax.nn.leaky_relu(alpha_s[src] + alpha_d[dst], NEG_SLOPE)
            m = jax.ops.segment_max(e, dst, num_segments=n_nodes)
            w = jnp.exp(e - m[dst])
            z = jax.ops.segment_sum(w, dst, num_segments=n_nodes)
            alpha = w / (z[dst] + 1e-16)
            out = jax.ops.segment_sum(alpha[:, None] * h[src], dst, num_segments=n_nodes)
            return out + b
        n_nodes = x.shape[0]
        loops = jnp.arange(n_nodes, dtype=edge_index.dtype)
        src = jnp.concatenate([edge_index[0], loops])
        dst = jnp.concatenate([edge_index[1], loops])
        h = _gat_layer(x, src, dst, n_nodes, W1, a_src1, a_dst1, b1)
        h = jax.nn.relu(h)
        out = _gat_layer(h, src, dst, n_nodes, W2, a_src2, a_dst2, b2)
        return out
    edge_index = jnp.stack([src, dst])
    h = jnp.maximum(_layernorm(x, axis=-1), 0.0)
    x = x + _L0_gnn_ref(h, edge_index, L0_gnn_alpha)
    h = jnp.maximum(_layernorm(x, axis=-1), 0.0)
    x = x + _L1_gnn_ref(h, L1_gnn_Wq, L1_gnn_Wk, L1_gnn_Wv, edge_index)
    h = jnp.maximum(_layernorm(x, axis=-1), 0.0)
    x = x + _L2_gnn_ref(h, edge_index)
    h = jnp.maximum(_layernorm(x, axis=-1), 0.0)
    x = x + _L3_gnn_ref(h, edge_index, L3_gnn_W1, L3_gnn_a_src1, L3_gnn_a_dst1, L3_gnn_b1, L3_gnn_W2, L3_gnn_a_src2, L3_gnn_a_dst2, L3_gnn_b2)
    return x

_drawn_inputs = setup_inputs


def setup_inputs(seed=0):
    import zlib

    import numpy as np

    out = dict(_drawn_inputs(seed))
    spreads = {'L0_gnn_alpha': (0.3333333432674408, 0.2),
     'L3_gnn_b1': (0.0, 0.1),
     'L3_gnn_b2': (0.0, 0.1)}
    factors = {'L3_gnn_a_dst1': 40.39, 'L3_gnn_a_src2': 28.506, 'L3_gnn_a_dst2': 52.443}
    for name, (base, spread) in spreads.items():
        noise = np.random.default_rng([zlib.crc32(name.encode()), seed]).standard_normal(out[name].shape)
        drawn = base * np.exp(spread * noise) if base else spread * noise
        out[name] = jnp.asarray(drawn.astype(out[name].dtype))
    for name, factor in factors.items():
        out[name] = (out[name] * factor).astype(out[name].dtype)
    return out
```

```python
from contextlib import ExitStack

import concourse.bass as bass
from concourse import mybir

P = 128
G = 2
CH = G * P
CB = 8
T = CB * G
S = 4
F = 64
HEADS = 4
DH = F // HEADS
KV = 2 * F
ROW = 133
BIG = 1.0e30
NO_NODE = 20000
PROJ = 5

f32 = mybir.dt.float32
bf16 = mybir.dt.bfloat16
i32 = mybir.dt.int32
u32 = mybir.dt.uint32
i16 = mybir.dt.int16
ALU = mybir.AluOpType
ACT = mybir.ActivationFunctionType
AX = mybir.AxisListType
DVE_ONLY = (mybir.EngineType.DVE,)
PE_ONLY = (mybir.EngineType.PE,)
SP_ONLY = (mybir.EngineType.SP,)


def gnn_kernel(nc, x_in, src_in, dst_in, alpha_in, wq_in, wk_in, wv_in,
               w1_in, as1_in, ad1_in, b1_in, w2_in, as2_in, ad2_in, b2_in, out):
    N = x_in.shape[0]
    E = src_in.shape[0]
    EP = E // P
    assert EP * P == E and N < 16384
    NBLK = -(-N // P)
    FULL = N // P
    TAIL = N - FULL * P
    NB = 2 * PROJ * (-(-(NBLK + 1) // (2 * PROJ)))
    assert NB <= P
    NCH = -(-(E + NBLK * (CH - 1)) // CH)
    NBAT = -(-NCH // CB)
    NBAT = S * (-(-NBAT // S))
    NC_ = (NBAT + S) * CB
    ITERS = NBAT // S
    SC = next(d for d in (25, 5, 1) if EP % d == 0)
    SC0 = -(-SC // 2)
    SCH = (SC0, SC - SC0)

    y_table = nc.dram_tensor("y_table", (NB * P, F), f32).ap()
    kv_table = nc.dram_tensor("kv_table", (NB * P, KV), f32).ap()
    g_table = nc.dram_tensor("g_table", (NB * P, F + 1), f32).ap()
    by_dst = nc.dram_tensor("by_dst", (E + CH, 2), i16).ap()
    by_src = nc.dram_tensor("by_src", (E + CH, 2), i16).ap()

    ctx = ExitStack()
    with ctx:
        def sb(name, shape, dt):
            return ctx.enter_context(nc.sbuf_tensor(name, shape, dt))

        def sem(name):
            return ctx.enter_context(nc.semaphore(name))

        xr = sb("xr", [P, NB * F], f32)
        accr = sb("accr", [P, max(NB * (F + HEADS + 1), 2 * EP)], f32)
        auxr = sb("auxr", [P, max(NB * F, 3 * NC_, 2 * EP)], f32)
        ROWS = S * T * ROW
        work = sb("work", [P, ROWS + 4 * T * P], f32)

        def view(region, at, shape, dt=f32):
            n = 1
            for s in shape:
                n *= s
            size = n * (2 if dt in (bf16, i16) else 4)
            v = region[:, at:at + -(-size // 4)]
            if dt != f32:
                v = v.bitcast(dt)
            v = v[:, 0:n]
            if len(shape) == 2:
                v = v.rearrange("p (a b) -> p a b", b=shape[1])
            if len(shape) == 3:
                v = v.rearrange("p (a b c) -> p a b c", b=shape[1], c=shape[2])
            return v

        x = view(xr, 0, [NB, F])
        acc64 = view(accr, 0, [NB, F])
        acc69 = view(accr, 0, [NB, F + HEADS + 1])
        acc65 = view(accr, 0, [NB, F + 1])
        aux = view(auxr, 0, [NB, F])
        src32 = view(xr, 0, [EP], i32)
        dst32 = view(xr, EP, [EP], i32)
        src_block = view(accr, 0, [EP])
        block_hit = view(accr, EP, [EP])
        block_int = view(accr, EP, [EP], i32)
        sorted_at = view(auxr, 0, [EP])
        src_pairs = view(auxr, EP, [EP, 2], i16)
        dst_block = view(work, 0, [EP])
        dst_pairs = view(work, EP, [EP, 2], i16)
        sign_out = view(work, 2 * EP, [EP])
        running = view(work, 3 * EP, [EP])
        AT = 4 * EP
        began = view(work, AT, [NC_])
        chunk_no = view(work, AT + NC_, [NC_])
        assert AT + 2 * NC_ <= ROWS + 4 * T * P
        centered = view(work, 0, [NB, F])
        squares = view(work, NB * F, [NB, F])
        y_stage = view(work, 0, [NB, F])
        kv_stage = view(work, 0, [NB, KV])
        g_stage = view(work, 0, [NB, F + 1])
        g_times = view(work, NB * (F + 1), [NB, F])
        block_hot = view(work, NB * (F + 1), [NC_])
        h_t = view(work, NB * KV, [PROJ * P])
        tab_t = view(work, NB * KV + PROJ * P, [2, P])
        h_stage = view(work, NB * KV + PROJ * P + 2 * P, [PROJ * P])
        rows = [view(work, s * T * ROW, [T, ROW]) for s in range(S)]
        hot = [view(work, ROWS + i * T * P, [T, P]) for i in range(4)]
        hot_bf = [view(work, ROWS + i * T * P, [T, P], bf16) for i in range(2)]
        onehot = hot[0:2]
        onehot_t = hot[2:4]
        nothot, scores, hot_e, hot_te = hot
        ad_chunk = view(auxr, 0, [NC_])
        self_chunk = view(auxr, NC_, [NC_])
        fresh = view(auxr, 2 * NC_, [NC_])

        pairs = [sb(f"pairs_{d}", [P, NC_, G, 2], i16) for d in ("by_dst", "by_src")]
        block128 = [sb(f"block128_{d}", [P, NC_], f32) for d in ("by_dst", "by_src")]
        chunk_int = sb("chunk_int", [P, NC_], i32)
        iota = sb("iota", [P, P], f32)
        ident = sb("ident", [P, P], f32)
        col_no = sb("col_no", [P, P], f32)
        before = sb("before", [P, P], f32)
        upto = sb("upto", [P, P], f32)
        ones = sb("ones", [P, P], f32)
        ones_bf = sb("ones_bf", [P, 1], bf16)
        half_up = sb("half_up", [P, P], f32)
        real128 = sb("real128", [P, P], f32)
        counts = [sb(f"counts_{d}", [P, P], f32) for d in ("by_dst", "by_src")]
        cumul = sb("cumul", [P, P + 1], f32)
        small = [sb(f"small{i}", [P, P], f32) for i in range(4)]
        col = [sb(f"col{i}", [P, 1], f32) for i in range(4)]
        col_int = sb("col_int", [P, 1], i32)
        delta_wide = sb("delta_wide", [P, P], f32)
        no_edge = sb("no_edge", [P, G, 2], i16)
        at_stage = [sb(f"at_stage{i}", [P, SC], i32) for i in range(2)]
        pair_stage = [sb(f"pair_stage{i}", [P, SC, 2], i16) for i in range(2)]
        index = [sb(f"index{s}", [P, T], i32) for s in range(S)]
        local = sb("local", [P, T], f32)
        dis_dst = sb("dis_dst", [P, NB], f32)
        dis_src = sb("dis_src", [P, NB], f32)
        mean = sb("mean", [P, NB], f32)
        rstd = sb("rstd", [P, NB], f32)
        alpha = sb("alpha", [P, 3], f32)
        vecs = [sb(n, [P, F], f32) for n in ("as1", "ad1", "b1", "as2", "ad2", "b2")]
        w_qkv = sb("w_qkv", [P, 2, 3 * F], f32)
        w_gat = [sb(f"w_gat{i}", [P, 2, F], f32) for i in range(2)]
        att = sb("att", [P, T * HEADS], f32)
        peak = [sb(f"peak{i}", [P, CB + 1], f32) for i in range(2)]
        chunk_max = sb("chunk_max", [P, CB], f32)
        leak = sb("leak", [P, CB], f32)
        fade_in = sb("fade_in", [P, CB], f32)
        fade = sb("fade", [P, CB], f32)
        node_pair = sb("node_pair", [P, CB, 2], f32)
        edge_a = sb("edge_a", [P, T], f32)
        edge_b = sb("edge_b", [P, T], f32)
        weight = sb("weight", [P, T], f32)
        ad_tab = sb("ad_tab", [P, P], f32)
        self_tab = sb("self_tab", [P, P], f32)

        psum = ctx.enter_context(nc.psum_tensor("psum", [P, 8, 512], f32))

        def banks(a, n):
            return psum[:, a:a + n, :].rearrange("p a b -> p (a b)")

        edges_in = sem("edges_in")
        weights_in = sem("weights_in")
        iotas = sem("iotas")
        consts = sem("consts")
        zeroed = sem("zeroed")
        keys_split = sem("keys_split")
        pairs_made = sem("pairs_made")
        pairs_out = sem("pairs_out")
        dst_counted = sem("dst_counted")
        counted = sem("counted")
        totals = sem("totals")
        columns = sem("columns")
        cum_cols = sem("cum_cols")
        began_ready = sem("began_ready")
        tables_psum = sem("tables_psum")
        tables_read = sem("tables_read")
        offsets_ready = sem("offsets_ready")
        places_ready = sem("places_ready")
        staged_pairs = sem("staged_pairs")
        scattered = [sem(f"scattered{i}") for i in range(2)]
        scattering = sem("scattering")
        gathering = sem("gathering")
        pairs_in = [sem(f"pairs_in_{d}") for d in ("by_dst", "by_src")]
        x_in_sem = sem("x_in_sem")
        x_region_free = sem("x_region_free")
        deg_hot = sem("deg_hot")
        deg_psum = sem("deg_psum")
        table_ready = [sem(f"table_ready{p}") for p in range(6)]
        table_out = [sem(f"table_out{p}") for p in range(6)]
        h_ready = [sem(f"h_ready{i}") for i in range(3)]
        h_staged = [sem(f"h_staged{i}") for i in range(3)]
        h_turned = [sem(f"h_turned{i}") for i in range(3)]
        h_t_ready = [sem(f"h_t_ready{i}") for i in range(3)]
        projected = [sem(f"projected{i}") for i in range(3)]
        proj_read = [sem(f"proj_read{i}") for i in range(3)]
        tabs_ready = [sem(f"tabs_ready{i}") for i in range(2)]
        tabs_turned = [sem(f"tabs_turned{i}") for i in range(2)]
        tabs_t_ready = [sem(f"tabs_t_ready{i}") for i in range(2)]
        spread_psum = [sem(f"spread_psum{i}") for i in range(2)]
        root_in = sem("root_in")
        root_out = sem("root_out")
        out_ready = sem("out_ready")
        out_done = sem("out_done")
        LINEAR = (0, 1, 3)
        TURNING = (2, 4, 5)

        def sems(name, passes=range(6)):
            return {p: sem(f"{name}{p}") for p in passes}

        staged = sems("staged")
        landed = [[sem(f"landed{p}_{s}") for s in range(S)] for p in range(6)]
        used = sems("used")
        summed = sems("summed")
        hot_ready = sems("hot_ready")
        added = {p: [sem(f"added{p}_{q}") for q in range(2 if p in LINEAR else 1)] for p in range(6)}
        turned = sems("turned", TURNING)
        turned_read = sems("turned_read", TURNING)
        nodes_ready = sems("nodes_ready", TURNING)
        spread = sems("spread", TURNING)
        exp_in = sems("exp_in", TURNING)
        exp_out = sems("exp_out", TURNING)
        rows_ready = sems("rows_ready", TURNING)
        fade_out = sems("fade_out", TURNING[1:])

        DIRECTION = (0, 0, 1, 1, 0, 0)
        TABLE = (y_table, y_table, kv_table, y_table, g_table, g_table)
        WIDTH = (F, F, KV, F, F + 1, F + 1)
        BLOCK_ROW = (0, 32)
        OFFSET_ROW = (64, 96)

        block = ctx.enter_context(nc.Block())

        @block.sync
        def _(sp):
            sp.dma_start(src32, src_in.rearrange("(p t) -> p t", t=EP)).then_inc(edges_in, 16)
            sp.dma_start(dst32, dst_in.rearrange("(p t) -> p t", t=EP)).then_inc(edges_in, 16)
            sp.dma_start(alpha[:, :], alpha_in.rearrange("(a n) -> a n", a=1).to_broadcast([P, 3]))\
              .then_inc(weights_in, 16)
            for v, a in zip(vecs, (as1_in, ad1_in, b1_in, as2_in, ad2_in, b2_in)):
                sp.dma_start(v[:, :], a.rearrange("(a n) -> a n", a=1).to_broadcast([P, F]))\
                  .then_inc(weights_in, 16)
            sp.wait_ge(zeroed, 1)
            for half in range(2):
                part = slice(half * F, half * F + F)
                for k, w in enumerate((wq_in, wk_in, wv_in)):
                    sp.dma_start(w_qkv[part, half, k * F:k * F + F], w).then_inc(weights_in, 16)
                sp.dma_start(w_gat[0][part, half, :], w1_in).then_inc(weights_in, 16)
                sp.dma_start(w_gat[1][part, half, :], w2_in).then_inc(weights_in, 16)
            sp.wait_ge(pairs_made, 1)
            sp.dma_start(by_dst[0:E, :].rearrange("(p t) c -> p t c", t=EP), dst_pairs)\
              .then_inc(pairs_out, 16)
            for table in (by_dst, by_src):
                sp.dma_start(table[E:E + CH, :].rearrange("(p g) c -> p g c", g=G), no_edge[:, :, :])\
                  .then_inc(pairs_out, 16)
            sp.wait_ge(x_region_free, 1)
            sp.dma_start(x[:, 0:FULL, :], x_in[0:FULL * P, :].rearrange("(b p) f -> p b f", p=P))\
              .then_inc(x_in_sem, 16)
            if TAIL:
                sp.dma_start(x[0:TAIL, FULL, :], x_in[FULL * P:N, :]).then_inc(x_in_sem, 16)

            def load_chunks(direction, table):
                with sp.Fori(0, NBAT + S) as n:
                    for k in range(CB):
                        at = sp.value_load(
                            chunk_int[OFFSET_ROW[direction]:OFFSET_ROW[direction] + 1,
                                      bass.ds(n * CB + k, 1)], min_val=0, max_val=E)
                        if k == 0:
                            sp.wait_ge(pairs_in[direction], n * (16 * CB))
                        sp.dma_start(
                            pairs[direction][:, bass.ds(n * CB + k, 1), :, :].rearrange("p o g c -> p (o g c)"),
                            table[bass.ds(at, CH), :].rearrange("(p g) c -> p (g c)", g=G))\
                          .then_inc(pairs_in[direction], 16)

            sp.wait_ge(offsets_ready, 1)
            sp.wait_ge(pairs_out, 48)
            load_chunks(0, by_dst)
            for i in range(2):
                sp.wait_ge(scattered[i], 16 * SCH[i] * (EP // SC))
            load_chunks(1, by_src)

            stages = (y_stage, y_stage, kv_stage, y_stage, g_stage, g_stage)
            for p in range(6):
                sp.wait_ge(table_ready[p], 1)
                sp.dma_start(TABLE[p].rearrange("(b p) f -> p b f", p=P), stages[p]).then_inc(table_out[p], 16)
            sp.wait_ge(out_ready, 1)
            sp.dma_start(out[0:FULL * P, :].rearrange("(b p) f -> p b f", p=P), x[:, 0:FULL, :])\
              .then_inc(out_done, 16)
            if TAIL:
                sp.dma_start(out[FULL * P:N, :], x[0:TAIL, FULL, :]).then_inc(out_done, 16)
            sp.wait_ge(out_done, 32 if TAIL else 16)

        @block.gpsimd
        def _(pool):
            nc.gpsimd.memset(w_qkv[:, :, :], 0.0)
            nc.gpsimd.memset(w_gat[0][:, :, :], 0.0)
            nc.gpsimd.memset(w_gat[1][:, :, :], 0.0)
            nc.gpsimd.memset(no_edge[:, :, 0:1], 0)
            nc.gpsimd.memset(no_edge[:, :, 1:2], NO_NODE)
            pool.drain()
            nc.gpsimd.memset(ones[:, :], 1.0).then_inc(zeroed, 1)
            nc.gpsimd.iota(iota[:, :], [[1, P]], base=0, channel_multiplier=0,
                           allow_small_or_imprecise_dtypes=True)
            nc.gpsimd.iota(col_no[:, :], [[0, P]], base=0, channel_multiplier=1,
                           allow_small_or_imprecise_dtypes=True)
            nc.gpsimd.iota(chunk_no, [[1, NC_]], base=0, channel_multiplier=0,
                           allow_small_or_imprecise_dtypes=True)
            nc.gpsimd.memset(ones_bf[:, :], 1.0)
            pool.drain()
            nc.gpsimd.memset(cumul[:, :], 0.0).then_inc(iotas, 1)

            pool.wait_ge(places_ready, 1)
            with pool.Fori(0, EP // SC) as i:
                for part in range(2):
                    if SCH[part]:
                        t0 = i * SC + part * SC0
                        n = SCH[part]
                        pool.wait_ge(scattered[part], i * (16 * n))
                        pool.sem_inc(scattering, 1)
                        nc.gpsimd.tensor_copy(at_stage[part][:, 0:n], sorted_at[:, bass.ds(t0, n)])
                        nc.gpsimd.tensor_copy(pair_stage[part][:, 0:n, :], src_pairs[:, bass.ds(t0, n), :])\
                          .then_inc(staged_pairs, 1)
                        pool.wait_ge(staged_pairs, i * sum(1 for c in SCH if c) + part + 1)
                        pool.sem_inc(scattering, 1)
                        for u in range(n):
                            nc.gpsimd.indirect_dma_start(
                                by_src,
                                bass.IndirectOffsetOnAxis(ap=at_stage[part][:, u:u + 1].bitcast(u32), axis=0),
                                pair_stage[part][:, u, :], None).then_inc(scattered[part], 16)

            for p in range(6):
                pool.wait_ge(table_out[p], 16)
                with pool.Fori(0, ITERS) as it:
                    for s in range(S):
                        pool.wait_ge(staged[p], it * S + s + 1)
                        pool.sem_inc(gathering, 1)
                        for t in range(T):
                            nc.gpsimd.indirect_dma_start(
                                rows[s][:, t, 0:WIDTH[p]], None, TABLE[p],
                                bass.IndirectOffsetOnAxis(ap=index[s][:, t:t + 1].bitcast(u32), axis=0))\
                              .then_inc(landed[p][s], 16)

        @block.scalar
        def _(act):
            act.wait_ge(consts, 1)
            act.wait_ge(keys_split, 1)
            with act.Fori(0, NBLK) as b:
                act.drain()
                nc.scalar.activation(sign_out, dst_block, ACT.Sign, bias=half_up[:, bass.ds(b, 1)],
                                     scale=-1.0, accum_out=cumul[:, bass.ds(b + 1, 1)])
            act.drain()
            nc.scalar.activation(mean[:, 0:1], ones[:, 0:1], ACT.Copy).then_inc(dst_counted, 1)

            def turn_h(i, h):
                with act.Fori(0, NB // (2 * PROJ)) as j:
                    act.wait_ge(h_ready[i], 1)
                    nc.scalar.activation(h_stage.rearrange("p (b f) -> p b f", f=F),
                                         h[:, bass.ds(j * (2 * PROJ), 2 * PROJ), :], ACT.Copy)\
                      .then_inc(h_staged[i], 1)
                    act.wait_ge(projected[i], j * PROJ)
                    act.wait_ge(h_turned[i], j + 1)
                    nc.scalar.activation(h_t, banks(0, 2)[:, 0:PROJ * P], ACT.Copy)\
                      .then_inc(h_t_ready[i], 1)

            def root(k):
                act.wait_ge(root_in, k)
                nc.scalar.activation(rstd[:, :], rstd[:, :], ACT.Sqrt).then_inc(root_out, 1)

            root(1)
            root(2)
            root(3)
            turn_h(0, acc64)
            p = 2
            act.wait_ge(turned[p], 1)
            nc.scalar.activation(onehot_t[0], banks(0, 4).rearrange("p (t n) -> p t n", n=P), ACT.Copy)\
              .then_inc(turned_read[p], 1)
            with act.Fori(0, ITERS) as it:
                for s in range(S):
                    act.wait_ge(exp_in[p], it * S + s + 1)
                    nc.scalar.activation(rows[s][:, :, KV:KV + HEADS],
                                         att[:, :].rearrange("p (t h) -> p t h", h=HEADS), ACT.Exp)\
                      .then_inc(exp_out[p], 1)
                    act.wait_ge(turned[p], it * S + s + 2)
                    nc.scalar.activation(onehot_t[(s + 1) % 2], banks(0, 4).rearrange("p (t n) -> p t n", n=P),
                                         ACT.Copy).then_inc(turned_read[p], 1)

            for k in (4, 5, 6):
                root(k)
            for i in range(2):
                turn_h(1 + i, aux)
                p = 4 + i
                with act.Fori(0, ITERS) as it:
                    for s in range(S):
                        n = it * S + s
                        act.wait_ge(hot_ready[p], n + 1)
                        act.wait_ge(used[p], n)
                        nc.scalar.activation(hot_e, nothot, ACT.Copy, bias=1.0, scale=-1.0)\
                          .then_inc(turned_read[p], 1)
                        act.wait_ge(nodes_ready[p], n + 1)
                        nc.scalar.activation(fade[:, :], fade_in[:, :], ACT.Exp).then_inc(fade_out[p], 1)
                        act.wait_ge(exp_in[p], n + 1)
                        nc.scalar.activation(weight[:, :], edge_b[:, :], ACT.Exp).then_inc(exp_out[p], 1)

        @block.tensor
        def _(pe):
            mm = nc.tensor.matmul
            for d in range(2):
                pe.wait_ge(counted, d + 1)
                mm(psum[:, d, 0:P], ones[:, :], counts[d][:, :], start=True, stop=True)
                mm(psum[:, d, P:2 * P], before[:, :], counts[d][:, :], start=True, stop=True)
                mm(psum[:, d, 2 * P:2 * P + 1], counts[d][:, :], ones[:, 0:1], start=True, stop=True)\
                    .then_inc(totals, 1)
                pe.wait_ge(columns, d + 1)
                mm(psum[:, d, 2 * P + 1:2 * P + 2], upto[:, :], col[1][:, :], start=True, stop=True)\
                    .then_inc(cum_cols, 1)
                pe.wait_ge(began_ready, d + 1)
                for j, c in enumerate(range(0, NC_, 512)):
                    w = min(512, NC_ - c)
                    if j or d:
                        pe.wait_ge(tables_read, d * len(range(0, NC_, 512)) + j)
                    mm(psum[:, 2, 0:w], real128[:, :], began[:, c:c + w], start=True, stop=True)
                    mm(psum[:, 3, 0:w], delta_wide[:, :], began[:, c:c + w], start=True, stop=True)\
                        .then_inc(tables_psum, 1)
            with pe.Fori(0, NBAT // 2) as n:
                for q in range(2):
                    pe.wait_ge(deg_hot, n * 2 + q + 1)
                    for k in range(CB):
                        for g in range(G):
                            last = mm(psum[:, 4 + q, k:k + 1], hot_bf[q][:, k * G + g, :], ones_bf[:, :],
                                      start=(g == 0), stop=(g == G - 1))
                    last.then_inc(deg_psum, 1)

            def linear(p):
                with pe.Fori(0, ITERS) as it:
                    for s in range(S):
                        q = s % 2
                        pe.wait_ge(hot_ready[p], it * S + s + 1)
                        pe.wait_ge(landed[p][s], it * (16 * T) + 16 * T)
                        pe.wait_ge(added[p][q], it * (CB * S // 2) + CB * (s // 2))
                        for k in range(CB):
                            for g in range(G):
                                last = mm(psum[:, 2 * q + k // 4, (k % 4) * F:(k % 4) * F + F], onehot[q][:, k * G + g, :],
                                          rows[s][:, k * G + g, 0:F], start=(g == 0), stop=(g == G - 1))
                            if k == CB // 2 - 1:
                                last.then_inc(summed[p], 1)
                            if k == CB - 1:
                                last.then_inc(used[p], 1)

            def project(i, w, width):
                with pe.Fori(0, NB // (2 * PROJ)) as j:
                    for k in range(PROJ):
                        if k == 0:
                            pe.wait_ge(h_staged[i], j + 1)
                        last = nc.tensor.transpose(banks(0, 2)[:, k * P:k * P + P],
                                                   h_stage[:, k * P:k * P + P], ident[:, :])
                    last.then_inc(h_turned[i], 1)
                    pe.wait_ge(h_t_ready[i], j + 1)
                    pe.wait_ge(proj_read[i], j * PROJ)
                    for k in range(PROJ):
                        mm(psum[:, 2 + k, 0:width], h_t[:, k * P:k * P + P], w, start=True, stop=True)\
                            .then_inc(projected[i], 1)

            linear(0)
            linear(1)

            pe.wait_ge(weights_in, 16 * 17)
            project(0, w_qkv[:, :, :].rearrange("p a b -> p (a b)"), 6 * F)
            p = 2

            def turn(buf):
                for t in range(T):
                    last = nc.tensor.transpose(banks(0, 4)[:, t * P:t * P + P], buf[:, t, :], ident[:, :])
                last.then_inc(turned[p], 1)

            pe.wait_ge(hot_ready[p], 1)
            pe.wait_ge(proj_read[0], PROJ * (NB // (2 * PROJ)))
            turn(onehot[0])
            with pe.Fori(0, ITERS) as it:
                for s in range(S):
                    q = s % 2
                    n = it * S + s
                    _, blocks = nc.values_load_multi_w_load_instructions(
                        chunk_int[BLOCK_ROW[1]:BLOCK_ROW[1] + 1, bass.ds(n * CB, CB)],
                        engines=PE_ONLY, min_val=0, max_val=NBLK,
                        skip_runtime_bounds_check_because="a count of blocks")
                    pe.wait_ge(turned_read[p], n + 1)
                    pe.wait_ge(spread[p], n)
                    for t in range(T):
                        last = mm(psum[:, 4 + t // 8, (t % 8) * F:(t % 8) * F + F], onehot_t[q][:, t, :],
                                  aux[:, bass.ds(blocks[t // G], 1), :].rearrange("p o f -> p (o f)"),
                                  start=True, stop=True)
                    last.then_inc(nodes_ready[p], 1)
                    pe.wait_ge(hot_ready[p], n + 2)
                    turn(onehot[1 - q])
                    pe.wait_ge(rows_ready[p], n + 1)
                    pe.wait_ge(added[p][0], n * CB)
                    for k in range(CB):
                        for g in range(G):
                            last = mm(psum[:, 6 + k // 4, (k % 4) * 69:(k % 4) * 69 + 69],
                                      onehot[q][:, k * G + g, :], rows[s][:, k * G + g, F:ROW],
                                      start=(g == 0), stop=(g == G - 1))
                        if k == CB // 2 - 1:
                            last.then_inc(summed[p], 1)
                        if k == CB - 1:
                            last.then_inc(used[p], 1)

            linear(3)

            for i in range(2):
                p = 4 + i
                project(1 + i, w_gat[i][:, :, :].rearrange("p a b -> p (a b)"), 2 * F)
                pe.wait_ge(tabs_ready[i], 1)
                nc.tensor.transpose(psum[:, 0, 0:P], ad_tab[:, :], ident[:, :])
                nc.tensor.transpose(psum[:, 0, P:2 * P], self_tab[:, :], ident[:, :]).then_inc(tabs_turned[i], 1)
                pe.wait_ge(tabs_t_ready[i], 1)
                pieces = list(range(0, NC_, 512))
                assert len(pieces) <= 4
                for side in range(2):
                    for j, c in enumerate(pieces):
                        w = min(512, NC_ - c)
                        last = mm(psum[:, side * 4 + j, 0:w], tab_t[:, side, :], block_hot[:, c:c + w],
                                  start=True, stop=True)
                last.then_inc(spread_psum[i], 1)
                with pe.Fori(0, ITERS) as it:
                    for s in range(S):
                        n = it * S + s
                        pe.wait_ge(rows_ready[p], n * 2 + 1)
                        for t in range(T):
                            last = nc.tensor.transpose(banks(0, 4)[:, t * P:t * P + P], scores[:, t, :], ident[:, :])
                        last.then_inc(turned[p], 1)
                        pe.wait_ge(nodes_ready[p], n + 1)
                        for t in range(T):
                            last = mm(psum[:, 4, 2 * t:2 * t + 2], hot_te[:, t, :], node_pair[:, t // G, :],
                                      start=True, stop=True)
                        last.then_inc(spread[p], 1)
                        pe.wait_ge(rows_ready[p], n * 2 + 2)
                        pe.wait_ge(turned_read[p], n + 1)
                        pe.wait_ge(added[p][0], n * CB)
                        for k in range(CB):
                            for g in range(G):
                                last = mm(psum[:, 5 + k // 4, (k % 4) * 65:(k % 4) * 65 + 65],
                                          hot_e[:, k * G + g, :], rows[s][:, k * G + g, 0:F + 1],
                                          start=(g == 0), stop=(g == G - 1))
                            if k == CB // 2 - 1:
                                last.then_inc(summed[p], 1)
                            if k == CB - 1:
                                last.then_inc(used[p], 1)

        @block.vector
        def _(dve):
            v = nc.vector

            def wide(a, shape):
                return a.to_broadcast(shape)

            dve.wait_ge(iotas, 1)
            v.tensor_tensor(ident[:, :], iota[:, :], col_no[:, :], ALU.is_equal)
            v.tensor_tensor(before[:, :], iota[:, :], col_no[:, :], ALU.is_gt)
            v.tensor_tensor(upto[:, :], iota[:, :], col_no[:, :], ALU.is_ge)
            v.tensor_scalar(real128[:, :], col_no[:, :], float(NBLK), float(P), ALU.is_lt, ALU.mult)
            v.tensor_scalar(half_up[:, :], iota[:, :], 0.5, None, ALU.add)
            dve.drain()
            v.memset(col[3][:, :], 0.0).then_inc(consts, 1)

            dve.wait_ge(edges_in, 32)
            v.tensor_scalar(block_int, dst32, 7, None, ALU.logical_shift_right)
            dve.drain()
            v.tensor_copy(dst_block, block_int).then_inc(keys_split, 1)
            v.tensor_copy(dst_pairs[:, :, 0], src32)
            v.tensor_copy(dst_pairs[:, :, 1], dst32)
            v.tensor_copy(src_pairs[:, :, 0], dst32)
            v.tensor_copy(src_pairs[:, :, 1], src32)
            dve.drain()
            v.memset(sorted_at, 0.0).then_inc(pairs_made, 1)
            v.tensor_scalar(block_int, src32, 7, None, ALU.logical_shift_right)
            dve.drain()
            v.tensor_copy(src_block, block_int)
            v.memset(counts[0][:, :], 0.0)
            v.memset(counts[1][:, :], 0.0)
            dve.drain()
            v.memset(xr[:, :], 0.0).then_inc(x_region_free, 1)
            with dve.Fori(0, NBLK) as b:
                dve.drain()
                v.tensor_scalar(block_hit, src_block, iota[:, bass.ds(b, 1)], 0.0, ALU.is_equal, ALU.add,
                                accum_out=counts[1][:, bass.ds(b, 1)])
            dve.wait_ge(dst_counted, 1)
            v.tensor_scalar(cumul[:, 1:NBLK + 1], cumul[:, 1:NBLK + 1], float(EP), 0.5, ALU.add, ALU.mult)
            dve.drain()
            v.tensor_tensor(counts[0][:, 0:NBLK], cumul[:, 1:NBLK + 1], cumul[:, 0:NBLK], ALU.subtract)
            dve.drain()

            for d in range(2):
                v.memset(col[3][:, :], 0.0).then_inc(counted, 1)
                dve.wait_ge(totals, d + 1)
                v.tensor_copy(col[0][:, :], psum[:, d, 2 * P:2 * P + 1])
                v.tensor_scalar(col_int[:, :], psum[:, d, 2 * P:2 * P + 1], float(CH - 1), None, ALU.add)
                dve.drain()
                v.tensor_scalar(col_int[:, :], col_int[:, :], CH.bit_length() - 1, None, ALU.logical_shift_right)
                dve.drain()
                v.tensor_copy(col[1][:, :], col_int[:, :])
                dve.drain()
                v.scalar_tensor_tensor(col[2][:, :], col[1][:, :], float(-CH), col[0][:, :], ALU.mult, ALU.add)\
                    .then_inc(columns, 1)
                dve.drain()
                if d:
                    dve.wait_ge(tables_psum, len(range(0, NC_, 512)))
                v.tensor_copy(delta_wide[:, :], wide(col[2][:, 0:1], [P, P]))
                dve.wait_ge(cum_cols, d + 1)
                v.tensor_copy(col[3][:, :], psum[:, d, 2 * P + 1:2 * P + 2])
                dve.drain()
                v.tensor_scalar(began, chunk_no, col[3][:, 0:1], None, ALU.is_ge)
                dve.drain()
                v.tensor_copy(small[3][:, 0:1], col[3][:, :]).then_inc(began_ready, 1)
                for j, c in enumerate(range(0, NC_, 512)):
                    w = min(512, NC_ - c)
                    dve.wait_ge(tables_psum, d * len(range(0, NC_, 512)) + j + 1)
                    v.tensor_copy(block128[d][:, c:c + w], psum[:, 2, 0:w])
                    r = BLOCK_ROW[d]
                    v.tensor_scalar(chunk_int[r:r + 1, c:c + w], psum[r:r + 1, 2, 0:w], 1.0 / P, None, ALU.mult)
                    r = OFFSET_ROW[d]
                    dve.drain()
                    v.scalar_tensor_tensor(running[r:r + 1, c:c + w], chunk_no[r:r + 1, c:c + w], float(CH),
                                           psum[r:r + 1, 3, 0:w], ALU.mult, ALU.add).then_inc(tables_read, 1)
                    dve.drain()
                    v.tensor_scalar(chunk_int[r:r + 1, c:c + w], running[r:r + 1, c:c + w], float(E), None, ALU.min)
            dve.drain()
            v.memset(col[3][:, :], 0.0).then_inc(offsets_ready, 1)

            v.memset(small[0][:, :], 0.0)
            v.tensor_copy(small[2][:, :], psum[:, 1, 0:P])
            dve.drain()
            v.tensor_tensor_scan(small[1][:, :], small[2][:, :], small[0][:, :], 0.0, ALU.add, ALU.add)
            dve.drain()
            v.scalar_tensor_tensor(small[1][:, :], small[1][:, :], -1.0, small[2][:, :], ALU.add, ALU.subtract)
            dve.drain()
            v.tensor_tensor(small[1][:, :], small[1][:, :], psum[:, 1, P:2 * P], ALU.add)
            dve.drain()
            with dve.Fori(0, NBLK) as b:
                v.tensor_scalar(block_hit, src_block, iota[:, bass.ds(b, 1)], None, ALU.is_equal)
                dve.drain()
                v.tensor_tensor_scan(running, block_hit, block_hit, small[1][:, bass.ds(b, 1)],
                                     ALU.add, ALU.bypass)
                dve.drain()
                v.copy_predicated(sorted_at, block_hit.bitcast(i32), running)
                dve.drain()
            v.memset(col[3][:, :], 0.0).then_inc(places_ready, 1)

            def load_blocks(direction, n):
                _, blocks = nc.values_load_multi_w_load_instructions(
                    chunk_int[BLOCK_ROW[direction]:BLOCK_ROW[direction] + 1, bass.ds(n * CB, CB)],
                    engines=DVE_ONLY, min_val=0, max_val=NBLK,
                    skip_runtime_bounds_check_because="a count of blocks")
                return blocks

            def keys_to_local(direction, n, drained=True):
                if drained:
                    dve.drain()
                v.tensor_tensor(local[:, :].rearrange("p (k g) -> p k g", g=G),
                                pairs[direction][:, bass.ds(n * CB, CB), :, 1],
                                wide(block128[direction][:, bass.ds(n * CB, CB)].unsqueeze(2), [P, CB, G]),
                                ALU.subtract)

            def compare(to, op):
                return v.tensor_tensor(to, wide(iota[:, :].unsqueeze(1), [P, T, P]),
                                       wide(local[:, :].unsqueeze(2), [P, T, P]), op)

            def stage_index(p, s, n):
                v.tensor_scalar(index[s][:, :].rearrange("p (k g) -> p k g", g=G),
                                pairs[DIRECTION[p]][:, bass.ds(n * CB, CB), :, 0], 0, None, ALU.add)\
                    .then_inc(staged[p], 1)

            deg = dis_dst
            v.memset(deg[:, :], 0.0)

            def add_deg(n, q):
                blocks = load_blocks(0, n)
                for k in range(CB):
                    dve.drain()
                    if k == 0:
                        dve.wait_ge(deg_psum, n + 1)
                    v.tensor_tensor(deg[:, bass.ds(blocks[k], 1)], deg[:, bass.ds(blocks[k], 1)],
                                    psum[:, 4 + q, k:k + 1], ALU.add)

            def deg_hots(n, q):
                dve.drain()
                dve.wait_ge(pairs_in[0], n * (16 * CB) + 16 * CB)
                keys_to_local(0, n, False)
                dve.drain()
                compare(hot_bf[q], ALU.is_equal).then_inc(deg_hot, 1)

            dve.wait_ge(pairs_out, 48)
            deg_hots(0, 0)
            with dve.Fori(0, NBAT // 2) as i:
                for q in range(2):
                    if q == 0:
                        deg_hots(i * 2 + 1, 1)
                    add_deg(i * 2 + q, q)
                    if q == 1:
                        deg_hots(i * 2 + 2, 0)
            dve.drain()

            roots = [0]

            def reciprocal_root():
                roots[0] += 1
                v.memset(col[3][:, :], 0.0).then_inc(root_in, 1)
                dve.wait_ge(root_out, roots[0])
                v.reciprocal(rstd[:, :], rstd[:, :])
                dve.drain()

            def inverse_root(t):
                v.tensor_scalar(mean[:, :], t[:, :], 0.0, None, ALU.is_gt)
                v.tensor_scalar(rstd[:, :], t[:, :], 1.0, None, ALU.max)
                dve.drain()
                reciprocal_root()
                v.tensor_tensor(t[:, :], mean[:, :], rstd[:, :], ALU.mult)
                dve.drain()

            def norm_relu(to):
                v.tensor_reduce(mean[:, :], x, AX.X, ALU.add)
                dve.drain()
                v.tensor_scalar(mean[:, :], mean[:, :], 1.0 / F, None, ALU.mult)
                dve.drain()
                v.tensor_tensor(centered, x, wide(mean[:, :].unsqueeze(2), [P, NB, F]), ALU.subtract)
                dve.drain()
                v.tensor_tensor(squares, centered, centered, ALU.mult)
                dve.drain()
                v.tensor_reduce(rstd[:, :], squares, AX.X, ALU.add)
                dve.drain()
                v.tensor_scalar(rstd[:, :], rstd[:, :], 1.0 / F, 1e-5, ALU.mult, ALU.add)
                dve.drain()
                reciprocal_root()
                last = v.scalar_tensor_tensor(to, centered, 0.0, wide(rstd[:, :].unsqueeze(2), [P, NB, F]),
                                              ALU.max, ALU.mult)
                return last

            def scaled(to, a, per_node):
                return v.tensor_tensor(to, a, wide(per_node.unsqueeze(2), [P, NB, F]), ALU.mult)

            def add_to_x(scalar, a):
                v.scalar_tensor_tensor(x, a, scalar, x, ALU.mult, ALU.add)

            def all_pairs_in(p):
                if DIRECTION[p]:
                    dve.wait_ge(pairs_in[1], (NBAT + S) * 16 * CB)
                else:
                    dve.wait_ge(pairs_in[0], (NBAT + S) * 16 * CB)

            def first_indices(p):
                all_pairs_in(p)
                for s in range(S):
                    stage_index(p, s, s)

            def linear(p):
                d = DIRECTION[p]
                first_indices(p)
                keys_to_local(d, 0)
                dve.drain()
                compare(onehot[0], ALU.is_equal).then_inc(hot_ready[p], 1)
                with dve.Fori(0, ITERS) as it:
                    for s in range(S):
                        q = s % 2
                        n = it * S + s
                        dve.drain()
                        keys_to_local(d, n + 1)
                        dve.drain()
                        compare(onehot[1 - q], ALU.is_equal).then_inc(hot_ready[p], 1)
                        blocks = load_blocks(d, n)
                        for k in range(CB):
                            dve.drain()
                            if k == 0:
                                dve.wait_ge(summed[p], n + 1)
                            if k == CB // 2:
                                dve.wait_ge(used[p], n + 1)
                            v.tensor_tensor(acc64[:, bass.ds(blocks[k], 1), :].rearrange("p o f -> p (o f)"),
                                            acc64[:, bass.ds(blocks[k], 1), :].rearrange("p o f -> p (o f)"),
                                            psum[:, 2 * q + k // 4, (k % 4) * F:(k % 4) * F + F], ALU.add).then_inc(added[p][q], 1)
                        stage_index(p, s, n + S)
                dve.drain()

            inverse_root(dis_dst)
            dve.wait_ge(x_in_sem, 32 if TAIL else 16)
            dve.wait_ge(weights_in, 16 * 17)
            norm_relu(acc64)
            dve.drain()
            add_to_x(alpha[:, 0:1], acc64)
            scaled(y_stage, acc64, dis_dst[:, :]).then_inc(table_ready[0], 1)
            dve.drain()
            v.memset(accr[:, :], 0.0)
            dve.drain()
            dve.wait_ge(table_out[0], 16)
            linear(0)
            scaled(acc64, acc64, dis_dst[:, :])
            dve.drain()
            add_to_x(alpha[:, 1:2], acc64)
            scaled(y_stage, acc64, dis_dst[:, :]).then_inc(table_ready[1], 1)
            dve.drain()
            v.memset(accr[:, :], 0.0)
            dve.drain()
            dve.wait_ge(table_out[1], 16)
            linear(1)
            scaled(acc64, acc64, dis_dst[:, :])
            dve.drain()
            add_to_x(alpha[:, 2:3], acc64)
            dve.drain()

            norm_relu(acc64)
            dve.drain()
            v.memset(col[3][:, :], 0.0).then_inc(h_ready[0], 1)
            with dve.Fori(0, NB // (2 * PROJ)) as j:
                for k in range(PROJ):
                    b2 = j * (2 * PROJ) + 2 * k
                    o = psum[:, 2 + k, 0:6 * F].rearrange("p (b f) -> p b f", b=2)
                    dve.wait_ge(projected[0], j * PROJ + k + 1)
                    v.tensor_scalar(aux[:, bass.ds(b2, 2), :], o[:, :, 0:F], 1.0, None, ALU.mult)
                    v.tensor_scalar(kv_stage[:, bass.ds(b2, 2), :], o[:, :, F:3 * F], 1.0, None, ALU.mult)\
                        .then_inc(proj_read[0], 1)
            dve.drain()
            v.memset(accr[:, :], 0.0).then_inc(table_ready[2], 1)
            dve.wait_ge(table_out[2], 16)
            p = 2
            for s in range(S):
                v.memset(rows[s][:, :, ROW - 1:ROW], 1.0)
            first_indices(p)
            keys_to_local(1, 0)
            dve.drain()
            compare(onehot[0], ALU.is_equal).then_inc(hot_ready[p], 1)

            def add_attention(n):
                blocks = load_blocks(1, n)
                for k in range(CB):
                    dve.drain()
                    if k == 0:
                        dve.wait_ge(summed[p], n + 1)
                    if k == CB // 2:
                        dve.wait_ge(used[p], n + 1)
                    a = acc69[:, bass.ds(blocks[k], 1), :].rearrange("p o f -> p (o f)")
                    v.tensor_tensor(a, a, psum[:, 6 + k // 4, (k % 4) * 69:(k % 4) * 69 + 69], ALU.add)\
                        .then_inc(added[p][0], 1)

            with dve.Fori(0, ITERS) as it:
                for s in range(S):
                    q = s % 2
                    n = it * S + s
                    prod = onehot_t[q]
                    prod = view(work, ROWS + (2 + q) * T * P, [T, F])
                    dve.wait_ge(landed[p][s], it * (16 * T) + 16 * T)
                    dve.wait_ge(nodes_ready[p], n + 1)
                    v.tensor_tensor(prod, rows[s][:, :, 0:F],
                                    banks(4, 2).rearrange("p (t f) -> p t f", f=F), ALU.mult)\
                        .then_inc(spread[p], 1)
                    dve.drain()
                    v.tensor_reduce(att[:, :], prod.rearrange("p t (h d) -> p (t h) d", d=DH), AX.X, ALU.add)
                    dve.drain()
                    v.tensor_scalar(att[:, :], att[:, :], -10.0, 10.0, ALU.max, ALU.min).then_inc(exp_in[p], 1)
                    keys_to_local(1, n + 1)
                    dve.drain()
                    compare(onehot[1 - q], ALU.is_equal).then_inc(hot_ready[p], 1)
                    dve.wait_ge(exp_out[p], n + 1)
                    vv = rows[s][:, :, F:KV].rearrange("p t (h d) -> p t h d", d=DH)
                    v.tensor_tensor(vv, vv, wide(rows[s][:, :, KV:KV + HEADS].unsqueeze(3), [P, T, HEADS, DH]),
                                    ALU.mult).then_inc(rows_ready[p], 1)
                    add_attention(n)
                    stage_index(p, s, n + S)
            dve.drain()

            v.tensor_copy(dis_src[:, :], acc69[:, :, F + HEADS])
            den = acc69[:, :, F:F + HEADS]
            v.tensor_scalar(den, den, 1e-8, None, ALU.add)
            dve.drain()
            v.reciprocal(den, den)
            dve.drain()
            num = acc69[:, :, 0:F].rearrange("p b (h d) -> p b h d", d=DH)
            v.tensor_tensor(num, num, wide(den.unsqueeze(3), [P, NB, HEADS, DH]), ALU.mult)
            dve.drain()
            v.tensor_tensor(x, x, acc69[:, :, 0:F], ALU.add)
            inverse_root(dis_src)

            norm_relu(acc64)
            dve.drain()
            scaled(y_stage, acc64, dis_src[:, :]).then_inc(table_ready[3], 1)
            dve.drain()
            v.memset(accr[:, :], 0.0)
            dve.drain()
            dve.wait_ge(table_out[3], 16)
            linear(3)
            scaled(acc64, acc64, dis_src[:, :])
            dve.drain()
            v.tensor_tensor(x, x, acc64, ALU.add)
            dve.drain()

            def gat(i, a_src, a_dst):
                p = 4 + i
                v.memset(col[3][:, :], 0.0).then_inc(h_ready[1 + i], 1)
                with dve.Fori(0, NB // (2 * PROJ)) as j:
                    for k in range(PROJ):
                        b2 = j * (2 * PROJ) + 2 * k
                        o = psum[:, 2 + k, 0:2 * F].rearrange("p (b f) -> p b f", b=2)
                        dve.wait_ge(projected[1 + i], j * PROJ + k + 1)
                        v.tensor_scalar(g_stage[:, bass.ds(b2, 2), 0:F], o, 1.0, None, ALU.mult)\
                            .then_inc(proj_read[1 + i], 1)
                dve.drain()
                g = g_stage[:, :, 0:F]
                v.memset(ad_tab[:, :], 0.0)
                v.memset(self_tab[:, :], 0.0)
                v.tensor_tensor(g_times, g, wide(a_src[:, :].unsqueeze(1), [P, NB, F]), ALU.mult)
                dve.drain()
                v.tensor_reduce(mean[:, :], g_times, AX.X, ALU.add)
                dve.drain()
                v.tensor_tensor(g_times, g, wide(a_dst[:, :].unsqueeze(1), [P, NB, F]), ALU.mult)
                dve.drain()
                v.tensor_reduce(ad_tab[:, 0:NB], g_times, AX.X, ALU.add)
                v.tensor_copy(g_stage[:, :, F], mean[:, :])
                dve.drain()
                v.tensor_tensor(rstd[:, :], mean[:, :], ad_tab[:, 0:NB], ALU.add)
                dve.drain()
                v.scalar_tensor_tensor(self_tab[:, 0:NB], rstd[:, :], 0.2, rstd[:, :], ALU.mult, ALU.max)
                v.tensor_copy(acc65[:, :, 0:F], g)
                v.memset(acc65[:, :, F:F + 1], 1.0)
                dve.drain()
                v.memset(col[3][:, :], 0.0).then_inc(table_ready[p], 1)
                v.tensor_scalar(block_hot, block128[0][:, :], 1.0 / P, col_no[:, 0:1], ALU.mult, ALU.is_equal)
                v.memset(fresh[:, 0:1], -BIG)
                v.tensor_tensor(fresh[:, 1:NC_], block128[0][:, 1:NC_], block128[0][:, 0:NC_ - 1], ALU.not_equal)
                dve.drain()
                v.tensor_scalar(fresh[:, 1:NC_], fresh[:, 1:NC_], -BIG, None, ALU.mult).then_inc(tabs_ready[i], 1)
                dve.wait_ge(tabs_turned[i], 1)
                v.tensor_copy(tab_t[:, :, :], psum[:, 0, 0:2 * P].rearrange("p (a b) -> p a b", a=2))\
                    .then_inc(tabs_t_ready[i], 1)
                dve.wait_ge(spread_psum[i], 1)
                v.tensor_copy(ad_chunk, banks(0, 4)[:, 0:NC_])
                v.tensor_copy(self_chunk, banks(4, 4)[:, 0:NC_])
                dve.wait_ge(table_out[p], 16)
                dve.drain()

                first_indices(p)
                v.memset(peak[1][:, :], -BIG)
                keys_to_local(0, 0)
                dve.drain()
                compare(nothot, ALU.not_equal).then_inc(hot_ready[p], 1)

                def add_chunks(n):
                    blocks = load_blocks(0, n)
                    for k in range(CB):
                        dve.drain()
                        if k == 0:
                            dve.wait_ge(summed[p], n + 1)
                        if k == CB // 2:
                            dve.wait_ge(used[p], n + 1)
                        a = acc65[:, bass.ds(blocks[k], 1), :].rearrange("p o f -> p (o f)")
                        v.scalar_tensor_tensor(a, a, fade[:, k:k + 1],
                                               psum[:, 5 + k // 4, (k % 4) * 65:(k % 4) * 65 + 65],
                                               ALU.mult, ALU.add).then_inc(added[p][0], 1)

                with dve.Fori(0, ITERS) as it:
                    for s in range(S):
                        q = s % 2
                        n = it * S + s
                        dve.drain()
                        dve.wait_ge(landed[p][s], it * (16 * T) + 16 * T)
                        v.scalar_tensor_tensor(scores, nothot, -BIG,
                                               wide(rows[s][:, :, F:F + 1], [P, T, P]), ALU.mult, ALU.add)\
                            .then_inc(rows_ready[p], 1)
                        dve.wait_ge(turned[p], n + 1)
                        v.tensor_reduce(chunk_max[:, :], banks(0, 4).rearrange("p (k e) -> p k e", k=CB),
                                        AX.X, ALU.max)
                        v.tensor_scalar(hot_te, banks(0, 4).rearrange("p (t e) -> p t e", t=T), -BIG / 2, None,
                                        ALU.is_gt)
                        ad_now = ad_chunk[:, bass.ds(n * CB, CB)]
                        self_now = self_chunk[:, bass.ds(n * CB, CB)]
                        fresh_now = fresh[:, bass.ds(n * CB, CB)]
                        dve.drain()
                        v.tensor_tensor(leak[:, :], chunk_max[:, :], ad_now, ALU.add)
                        v.tensor_scalar(node_pair[:, :, 0], ad_now, 1.0, None, ALU.mult)
                        dve.drain()
                        v.scalar_tensor_tensor(leak[:, :], leak[:, :], 0.2, leak[:, :], ALU.mult, ALU.max)
                        v.tensor_copy(peak[q][:, 0:1], peak[1 - q][:, CB:CB + 1])
                        dve.drain()
                        v.tensor_tensor(leak[:, :], leak[:, :], self_now, ALU.max)
                        dve.drain()
                        v.tensor_tensor_scan(peak[q][:, 1:CB + 1], fresh_now, leak[:, :], peak[q][:, 0:1],
                                             ALU.add, ALU.max)
                        dve.drain()
                        v.tensor_copy(node_pair[:, :, 1], peak[q][:, 1:CB + 1])
                        v.tensor_tensor(fade_in[:, :], peak[q][:, 0:CB], fresh_now, ALU.add)
                        dve.drain()
                        v.tensor_tensor(fade_in[:, :], fade_in[:, :], self_now, ALU.max)
                        dve.drain()
                        v.tensor_tensor(fade_in[:, :], fade_in[:, :], peak[q][:, 1:CB + 1], ALU.subtract)\
                            .then_inc(nodes_ready[p], 1)
                        keys_to_local(0, n + 1)
                        dve.drain()
                        dve.wait_ge(turned_read[p], n + 1)
                        compare(nothot, ALU.not_equal).then_inc(hot_ready[p], 1)
                        dve.wait_ge(spread[p], n + 1)
                        pair = psum[:, 4, 0:2 * T].rearrange("p (t c) -> p t c", c=2)
                        v.tensor_tensor(edge_a[:, :], rows[s][:, :, F], pair[:, :, 0], ALU.add)
                        dve.drain()
                        v.scalar_tensor_tensor(edge_a[:, :], edge_a[:, :], 0.2, edge_a[:, :], ALU.mult, ALU.max)
                        dve.drain()
                        v.tensor_tensor(edge_a[:, :], edge_a[:, :], pair[:, :, 1], ALU.subtract)
                        dve.drain()
                        v.tensor_scalar(edge_b[:, :], edge_a[:, :], 0.0, None, ALU.min).then_inc(exp_in[p], 1)
                        dve.wait_ge(exp_out[p], n + 1)
                        v.tensor_tensor(rows[s][:, :, 0:F], rows[s][:, :, 0:F],
                                        wide(weight[:, :].unsqueeze(2), [P, T, F]), ALU.mult)
                        v.tensor_copy(rows[s][:, :, F], weight[:, :])
                        dve.drain()
                        v.memset(col[3][:, :], 0.0).then_inc(rows_ready[p], 1)
                        dve.wait_ge(fade_out[p], n + 1)
                        add_chunks(n)
                        stage_index(p, s, n + S)
                dve.drain()
                den = acc65[:, :, F]
                v.tensor_scalar(mean[:, :], den, 1e-16, None, ALU.add)
                dve.drain()
                v.reciprocal(mean[:, :], mean[:, :])
                dve.drain()
                scaled(aux, acc65[:, :, 0:F], mean[:, :])
                dve.drain()

            norm_relu(aux)
            dve.drain()
            gat(0, vecs[0], vecs[1])
            v.tensor_tensor(aux, aux, wide(vecs[2][:, :].unsqueeze(1), [P, NB, F]), ALU.add)
            dve.drain()
            v.tensor_scalar(aux, aux, 0.0, None, ALU.max)
            dve.drain()
            gat(1, vecs[3], vecs[4])
            v.tensor_tensor(x, x, wide(vecs[5][:, :].unsqueeze(1), [P, NB, F]), ALU.add)
            dve.drain()
            v.tensor_tensor(x, x, aux, ALU.add).then_inc(out_ready, 1)


_INS = ['x', 'src', 'dst', 'L0_gnn_alpha', 'L1_gnn_Wq', 'L1_gnn_Wk', 'L1_gnn_Wv', 'L3_gnn_W1', 'L3_gnn_a_src1',
        'L3_gnn_a_dst1', 'L3_gnn_b1', 'L3_gnn_W2', 'L3_gnn_a_src2', 'L3_gnn_a_dst2', 'L3_gnn_b2']


def kernel(**inputs):
    import numpy as _np
    import concourse.bacc as _bacc
    from concourse.bass_utils import run_bass_kernel_spmd as _run

    nc = _bacc.Bacc("TRN2", target_bir_lowering=False, num_devices=1)
    arrays, args = {}, []
    for name in _INS:
        a = _np.ascontiguousarray(inputs[name])
        arrays[f"in_{name}_dram"] = a
        args.append(nc.dram_tensor(f"in_{name}_dram", a.shape, mybir.dt.from_np(a.dtype), kind="ExternalInput").ap())
    out = nc.dram_tensor("out_0_dram", arrays["in_x_dram"].shape, f32, kind="ExternalOutput").ap()
    gnn_kernel(nc, *args, out)
    r = _run(nc, [arrays], core_ids=[0])
    return r.results[0]["out_0_dram"]
```

```python
from contextlib import ExitStack

import concourse.bass as bass
from concourse import mybir

P = 128
G = 2
CH = G * P
CB = 8
T = CB * G
S = 4
F = 64
HEADS = 4
DH = F // HEADS
KV = 2 * F
ROW = 133
BIG = 1.0e30
NO_NODE = 20000
PROJ = 5

f32 = mybir.dt.float32
bf16 = mybir.dt.bfloat16
i32 = mybir.dt.int32
u32 = mybir.dt.uint32
i16 = mybir.dt.int16
ALU = mybir.AluOpType
ACT = mybir.ActivationFunctionType
AX = mybir.AxisListType
DVE_ONLY = (mybir.EngineType.DVE,)
PE_ONLY = (mybir.EngineType.PE,)
SP_ONLY = (mybir.EngineType.SP,)


def gnn_kernel(nc, x_in, src_in, dst_in, alpha_in, wq_in, wk_in, wv_in,
               w1_in, as1_in, ad1_in, b1_in, w2_in, as2_in, ad2_in, b2_in, out):
    N = x_in.shape[0]
    E = src_in.shape[0]
    EP = E // P
    assert EP * P == E and N < 16384
    NBLK = -(-N // P)
    FULL = N // P
    TAIL = N - FULL * P
    NB = 2 * PROJ * (-(-(NBLK + 1) // (2 * PROJ)))
    assert NB <= P
    NCH = -(-(E + NBLK * (CH - 1)) // CH)
    NBAT = -(-NCH // CB)
    NBAT = S * (-(-NBAT // S))
    NC_ = (NBAT + S) * CB
    ITERS = NBAT // S
    SC = next(d for d in (25, 5, 1) if EP % d == 0)
    SC0 = -(-SC // 2)
    SCH = (SC0, SC - SC0)
    units = EP // SC
    cuts = sorted({0, -(-units // 8), -(-units * 4 // 9), units})
    SEGMENTS = list(zip(cuts, cuts[1:]))

    y_table = nc.dram_tensor("y_table", (NB * P, F), f32).ap()
    kv_table = nc.dram_tensor("kv_table", (NB * P, KV), f32).ap()
    g_table = nc.dram_tensor("g_table", (NB * P, F + 1), f32).ap()
    by_dst = nc.dram_tensor("by_dst", (E + CH, 2), i16).ap()
    by_src = nc.dram_tensor("by_src", (E + CH, 2), i16).ap()

    ctx = ExitStack()
    with ctx:
        def sb(name, shape, dt):
            return ctx.enter_context(nc.sbuf_tensor(name, shape, dt))

        def sem(name):
            return ctx.enter_context(nc.semaphore(name))

        xr = sb("xr", [P, NB * F], f32)
        accr = sb("accr", [P, max(NB * (F + HEADS + 1), 2 * EP)], f32)
        auxr = sb("auxr", [P, max(NB * F, 3 * NC_, 2 * EP)], f32)
        ROWS = S * T * ROW
        work = sb("work", [P, ROWS + 4 * T * P], f32)

        def view(region, at, shape, dt=f32):
            n = 1
            for s in shape:
                n *= s
            size = n * (2 if dt in (bf16, i16) else 4)
            v = region[:, at:at + -(-size // 4)]
            if dt != f32:
                v = v.bitcast(dt)
            v = v[:, 0:n]
            if len(shape) == 2:
                v = v.rearrange("p (a b) -> p a b", b=shape[1])
            if len(shape) == 3:
                v = v.rearrange("p (a b c) -> p a b c", b=shape[1], c=shape[2])
            return v

        x = view(xr, 0, [NB, F])
        acc64 = view(accr, 0, [NB, F])
        acc69 = view(accr, 0, [NB, F + HEADS + 1])
        acc65 = view(accr, 0, [NB, F + 1])
        aux = view(auxr, 0, [NB, F])
        src32 = view(xr, 0, [EP], i32)
        dst32 = view(xr, EP, [EP], i32)
        src_block = view(accr, 0, [EP], bf16)
        block_hit = view(accr, EP, [EP])
        block_hit_bf = view(accr, EP, [EP], bf16)
        block_int = view(accr, EP, [EP], i32)
        sorted_at = view(auxr, 0, [EP])
        src_pairs = view(auxr, EP, [EP, 2], i16)
        dst_block = view(work, 0, [EP])
        dst_pairs = view(work, EP, [EP, 2], i16)
        sign_out = view(work, 2 * EP, [EP])
        running = view(work, 3 * EP, [EP])
        AT = 4 * EP
        began = view(work, AT, [NC_])
        chunk_no = view(work, AT + NC_, [NC_])
        assert AT + 2 * NC_ <= ROWS + 4 * T * P
        centered = view(work, 0, [NB, F])
        squares = view(work, NB * F, [NB, F])
        y_stage = view(work, 0, [NB, F])
        kv_stage = view(work, 0, [NB, KV])
        g_stage = view(work, 0, [NB, F + 1])
        g_times = view(work, NB * (F + 1), [NB, F])
        block_hot = view(work, NB * (F + 1), [NC_])
        h_t = view(work, NB * KV, [PROJ * P])
        tab_t = view(work, NB * KV + PROJ * P, [2, P])
        h_stage = view(work, NB * KV + PROJ * P + 2 * P, [PROJ * P])
        rows = [view(work, s * T * ROW, [T, ROW]) for s in range(S)]
        hot = [view(work, ROWS + i * T * P, [T, P]) for i in range(4)]
        hot_bf = [view(work, ROWS + i * T * P, [T, P], bf16) for i in range(2)]
        onehot = hot[0:2]
        onehot_bf = [view(work, ROWS + i * (T * P // 2), [T, P], bf16) for i in range(2)]
        onehot_t = [view(work, ROWS + (1 + i) * T * P, [T, P]) for i in range(2)]
        MSG = F + HEADS + 1
        products = view(work, ROWS + 3 * T * P, [T, F])
        rest = view(work, ROWS + 3 * T * P, [T, MSG])
        last_part = view(work, ROWS + 3 * T * P + T * MSG, [T, MSG], bf16)
        ROWS_E = S * T * (F + 1)
        rows_e = [view(work, s * T * (F + 1), [T, F + 1]) for s in range(S)]
        nothot = [view(work, ROWS_E + i * (T * P // 2), [T, P], bf16) for i in range(2)]
        scores = view(work, ROWS_E + T * P, [T, P])
        hot_e = [view(work, ROWS_E + (2 + i) * T * P, [T, P]) for i in range(2)]
        hot_te = view(work, ROWS_E + 4 * T * P, [T, P], bf16)
        assert ROWS_E + 5 * T * P <= ROWS + 4 * T * P

        def upper(a):
            names = "abcd"[:len(a.shape) - 1]
            outer, inner = " ".join(names[:-1]), names[-1]
            return a.bitcast(bf16).rearrange(f"p {outer} ({inner} w) -> p {outer} {inner} w", w=2)[..., 1]

        ad_chunk = view(auxr, 0, [NC_])
        self_chunk = view(auxr, NC_, [NC_])
        fresh = view(auxr, 2 * NC_, [NC_])

        pairs = [sb(f"pairs_{d}", [P, NC_, G, 2], i16) for d in ("by_dst", "by_src")]
        block128 = [sb(f"block128_{d}", [P, NC_], f32) for d in ("by_dst", "by_src")]
        chunk_int = sb("chunk_int", [P, NC_], i32)
        iota = sb("iota", [P, P], f32)
        ident = sb("ident", [P, P], f32)
        ident_bf = sb("ident_bf", [P, P], bf16)
        col_no = sb("col_no", [P, P], f32)
        before = sb("before", [P, P], f32)
        upto = sb("upto", [P, P], f32)
        ones = sb("ones", [P, P], f32)
        ones_bf = sb("ones_bf", [P, 1], bf16)
        half_up = sb("half_up", [P, P], f32)
        real128 = sb("real128", [P, P], f32)
        counts = [sb(f"counts_{d}", [P, P], f32) for d in ("by_dst", "by_src")]
        cumul = sb("cumul", [P, P + 1], f32)
        small = [sb(f"small{i}", [P, P], f32) for i in range(4)]
        col = [sb(f"col{i}", [P, 1], f32) for i in range(4)]
        col_int = sb("col_int", [P, 1], i32)
        delta_wide = sb("delta_wide", [P, P], f32)
        no_edge = sb("no_edge", [P, G, 2], i16)
        at_stage = [sb(f"at_stage{i}", [P, SC], i32) for i in range(2)]
        pair_stage = [sb(f"pair_stage{i}", [P, SC, 2], i16) for i in range(2)]
        index = [sb(f"index{s}", [P, T], i32) for s in range(S)]
        local = sb("local", [P, T], bf16)
        iota_bf = sb("iota_bf", [P, P], bf16)
        dis_dst = sb("dis_dst", [P, NB], f32)
        dis_src = sb("dis_src", [P, NB], f32)
        mean = sb("mean", [P, NB], f32)
        rstd = sb("rstd", [P, NB], f32)
        alpha = sb("alpha", [P, 3], f32)
        vecs = [sb(n, [P, F], f32) for n in ("as1", "ad1", "b1", "as2", "ad2", "b2")]
        w_qkv = sb("w_qkv", [P, 2, 3 * F], f32)
        w_gat = [sb(f"w_gat{i}", [P, 2, F], f32) for i in range(2)]
        att = sb("att", [P, T * HEADS], f32)
        peak = [sb(f"peak{i}", [P, CB + 1], f32) for i in range(2)]
        chunk_max = sb("chunk_max", [P, CB], f32)
        leak = sb("leak", [P, CB], f32)
        fade_in = sb("fade_in", [P, CB], f32)
        fade = [sb(f"fade{i}", [P, CB], f32) for i in range(2)]
        node_pair = [sb(f"node_pair{i}", [P, CB, 2], f32) for i in range(3)]
        edge_a = sb("edge_a", [P, T], f32)
        edge_b = sb("edge_b", [P, T], f32)
        weight = sb("weight", [P, T], f32)
        ad_tab = sb("ad_tab", [P, P], f32)
        self_tab = sb("self_tab", [P, P], f32)

        psum = ctx.enter_context(nc.psum_tensor("psum", [P, 8, 512], f32))

        def banks(a, n):
            return psum[:, a:a + n, :].rearrange("p a b -> p (a b)")

        turned_hot = banks(0, 2).bitcast(bf16).rearrange("p (t n) -> p t n", n=P)

        edges_in = sem("edges_in")
        weights_in = sem("weights_in")
        iotas = sem("iotas")
        consts = sem("consts")
        zeroed = sem("zeroed")
        keys_split = sem("keys_split")
        pairs_made = sem("pairs_made")
        pairs_out = sem("pairs_out")
        dst_counted = sem("dst_counted")
        counted = sem("counted")
        totals = sem("totals")
        columns = sem("columns")
        cum_cols = sem("cum_cols")
        began_ready = sem("began_ready")
        tables_psum = sem("tables_psum")
        tables_read = sem("tables_read")
        offsets_ready = sem("offsets_ready")
        places_ready = sem("places_ready")
        staged_pairs = sem("staged_pairs")
        scattered = [sem(f"scattered{i}") for i in range(2)]
        scattering = sem("scattering")
        gathering = sem("gathering")
        pairs_in = [sem(f"pairs_in_{d}") for d in ("by_dst", "by_src")]
        loaded = [sem(f"loaded_{d}") for d in ("by_dst", "by_src")]
        x_in_sem = sem("x_in_sem")
        x_region_free = sem("x_region_free")
        deg_hot = sem("deg_hot")
        deg_psum = sem("deg_psum")
        table_ready = [sem(f"table_ready{p}") for p in range(6)]
        table_out = [sem(f"table_out{p}") for p in range(6)]
        h_ready = [sem(f"h_ready{i}") for i in range(3)]
        h_staged = [sem(f"h_staged{i}") for i in range(3)]
        h_turned = [sem(f"h_turned{i}") for i in range(3)]
        h_t_ready = [sem(f"h_t_ready{i}") for i in range(3)]
        projected = [sem(f"projected{i}") for i in range(3)]
        proj_read = [sem(f"proj_read{i}") for i in range(3)]
        tabs_ready = [sem(f"tabs_ready{i}") for i in range(2)]
        tabs_turned = [sem(f"tabs_turned{i}") for i in range(2)]
        tabs_t_ready = [sem(f"tabs_t_ready{i}") for i in range(2)]
        spread_psum = [sem(f"spread_psum{i}") for i in range(2)]
        root_in = sem("root_in")
        root_out = sem("root_out")
        out_ready = sem("out_ready")
        out_done = sem("out_done")
        LINEAR = (0, 1, 3)
        TURNING = (2, 4, 5)

        def sems(name, passes=range(6)):
            return {p: sem(f"{name}{p}") for p in passes}

        staged = sems("staged")
        landed = [[sem(f"landed{p}_{s}") for s in range(S)] for p in range(6)]
        used = sems("used")
        summed = sems("summed")
        hot_ready = sems("hot_ready")
        added = {p: [sem(f"added{p}_{q}") for q in range(2 if p in LINEAR else 1)] for p in range(6)}
        turned = sems("turned", TURNING)
        turned_read = sems("turned_read", TURNING)
        nodes_ready = sems("nodes_ready", TURNING)
        spread = sems("spread", TURNING)
        exp_in = sems("exp_in", TURNING)
        exp_out = sems("exp_out", TURNING)
        rows_ready = sems("rows_ready", TURNING)
        fade_out = sems("fade_out", TURNING[1:])
        scores_ready = sems("scores_ready", TURNING[1:])

        DIRECTION = (0, 0, 1, 1, 0, 0)
        TABLE = (y_table, y_table, kv_table, y_table, g_table, g_table)
        WIDTH = (F, F, KV, F, F + 1, F + 1)
        BLOCK_ROW = (0, 32)
        OFFSET_ROW = (64, 96)

        block = ctx.enter_context(nc.Block())

        @block.sync
        def _(sp):
            sp.dma_start(src32, src_in.rearrange("(p t) -> p t", t=EP)).then_inc(edges_in, 16)
            sp.dma_start(dst32, dst_in.rearrange("(p t) -> p t", t=EP)).then_inc(edges_in, 16)
            sp.dma_start(alpha[:, :], alpha_in.rearrange("(a n) -> a n", a=1).to_broadcast([P, 3]))\
              .then_inc(weights_in, 16)
            for v, a in zip(vecs, (as1_in, ad1_in, b1_in, as2_in, ad2_in, b2_in)):
                sp.dma_start(v[:, :], a.rearrange("(a n) -> a n", a=1).to_broadcast([P, F]))\
                  .then_inc(weights_in, 16)
            sp.wait_ge(zeroed, 1)
            for half in range(2):
                part = slice(half * F, half * F + F)
                for k, w in enumerate((wq_in, wk_in, wv_in)):
                    sp.dma_start(w_qkv[part, half, k * F:k * F + F], w).then_inc(weights_in, 16)
                sp.dma_start(w_gat[0][part, half, :], w1_in).then_inc(weights_in, 16)
                sp.dma_start(w_gat[1][part, half, :], w2_in).then_inc(weights_in, 16)
            sp.wait_ge(pairs_made, 1)
            sp.dma_start(by_dst[0:E, :].rearrange("(p t) c -> p t c", t=EP), dst_pairs)\
              .then_inc(pairs_out, 16)
            for table in (by_dst, by_src):
                sp.dma_start(table[E:E + CH, :].rearrange("(p g) c -> p g c", g=G), no_edge[:, :, :])\
                  .then_inc(pairs_out, 16)
            sp.wait_ge(x_region_free, 1)
            sp.dma_start(x[:, 0:FULL, :], x_in[0:FULL * P, :].rearrange("(b p) f -> p b f", p=P))\
              .then_inc(x_in_sem, 16)
            if TAIL:
                sp.dma_start(x[0:TAIL, FULL, :], x_in[FULL * P:N, :]).then_inc(x_in_sem, 16)

            def load_chunks(direction, table):
                with sp.Fori(0, NBAT + S) as n:
                    for k in range(CB):
                        at = sp.value_load(
                            chunk_int[OFFSET_ROW[direction]:OFFSET_ROW[direction] + 1,
                                      bass.ds(n * CB + k, 1)], min_val=0, max_val=E)
                        sp.dma_start(
                            pairs[direction][:, bass.ds(n * CB + k, 1), :, :].rearrange("p o g c -> p (o g c)"),
                            table[bass.ds(at, CH), :].rearrange("(p g) c -> p (g c)", g=G))\
                          .then_inc(pairs_in[direction], 16)
                    sp.wait_ge(pairs_in[direction], n * (16 * CB) + 16 * CB)
                    sp.sem_inc(loaded[direction], 1)

            sp.wait_ge(offsets_ready, 1)
            sp.wait_ge(pairs_out, 48)
            load_chunks(0, by_dst)
            for i in range(2):
                sp.wait_ge(scattered[i], 16 * SCH[i] * (EP // SC))
            sp.wait_ge(offsets_ready, 2)
            load_chunks(1, by_src)

            sp.wait_ge(out_ready, 1)
            sp.dma_start(out[0:FULL * P, :].rearrange("(b p) f -> p b f", p=P), x[:, 0:FULL, :])\
              .then_inc(out_done, 16)
            if TAIL:
                sp.dma_start(out[FULL * P:N, :], x[0:TAIL, FULL, :]).then_inc(out_done, 16)
            sp.wait_ge(out_done, 32 if TAIL else 16)

        @block.gpsimd
        def _(pool):
            nc.gpsimd.memset(w_qkv[:, :, :], 0.0)
            nc.gpsimd.memset(w_gat[0][:, :, :], 0.0)
            nc.gpsimd.memset(w_gat[1][:, :, :], 0.0)
            nc.gpsimd.memset(no_edge[:, :, 0:1], 0)
            nc.gpsimd.memset(no_edge[:, :, 1:2], NO_NODE)
            pool.drain()
            nc.gpsimd.memset(ones[:, :], 1.0).then_inc(zeroed, 1)
            nc.gpsimd.iota(iota[:, :], [[1, P]], base=0, channel_multiplier=0,
                           allow_small_or_imprecise_dtypes=True)
            nc.gpsimd.iota(col_no[:, :], [[0, P]], base=0, channel_multiplier=1,
                           allow_small_or_imprecise_dtypes=True)
            nc.gpsimd.iota(chunk_no, [[1, NC_]], base=0, channel_multiplier=0,
                           allow_small_or_imprecise_dtypes=True)
            nc.gpsimd.iota(iota_bf[:, :], [[1, P]], base=0, channel_multiplier=0,
                           allow_small_or_imprecise_dtypes=True)
            nc.gpsimd.memset(ones_bf[:, :], 1.0)
            pool.drain()
            nc.gpsimd.memset(cumul[:, :], 0.0).then_inc(iotas, 1)

            def scatter(i, first):
                for part in range(2):
                    n = SCH[part]
                    if n:
                        t0 = i * SC + part * SC0
                        if not first:
                            pool.wait_ge(scattered[part], i * (16 * n))
                            pool.sem_inc(scattering, 1)
                        nc.gpsimd.tensor_copy(at_stage[part][:, 0:n], sorted_at[:, bass.ds(t0, n)])
                        nc.gpsimd.tensor_copy(pair_stage[part][:, 0:n, :], src_pairs[:, bass.ds(t0, n), :])\
                          .then_inc(staged_pairs, 1)
                        pool.wait_ge(staged_pairs, i * sum(1 for c in SCH if c) + part + 1)
                        pool.sem_inc(scattering, 1)
                        for u in range(n):
                            nc.gpsimd.indirect_dma_start(
                                by_src,
                                bass.IndirectOffsetOnAxis(ap=at_stage[part][:, u:u + 1].bitcast(u32), axis=0),
                                pair_stage[part][:, u, :], None).then_inc(scattered[part], 16)

            for g, (lo, hi) in enumerate(SEGMENTS):
                pool.wait_ge(places_ready, g + 1)
                if lo == 0:
                    scatter(0, True)
                    lo = 1
                if lo < hi:
                    with pool.Fori(lo, hi) as i:
                        scatter(i, False)

            for p in range(6):
                pool.wait_ge(table_out[p], 16)
                with pool.Fori(0, ITERS) as it:
                    for s in range(S):
                        pool.wait_ge(staged[p], it * S + s + 1)
                        pool.sem_inc(gathering, 1)
                        for t in range(T):
                            nc.gpsimd.indirect_dma_start(
                                (rows_e if p >= 4 else rows)[s][:, t, 0:WIDTH[p]], None, TABLE[p],
                                bass.IndirectOffsetOnAxis(ap=index[s][:, t:t + 1].bitcast(u32), axis=0))\
                              .then_inc(landed[p][s], 16)

        @block.scalar
        def _(act):
            act.wait_ge(consts, 1)
            act.wait_ge(keys_split, 1)
            with act.Fori(0, NBLK) as b:
                act.drain()
                nc.scalar.activation(sign_out, dst_block, ACT.Sign, bias=half_up[:, bass.ds(b, 1)],
                                     scale=-1.0, accum_out=cumul[:, bass.ds(b + 1, 1)])
            act.drain()
            nc.scalar.activation(mean[:, 0:1], ones[:, 0:1], ACT.Copy).then_inc(dst_counted, 1)

            def turn_h(i, h):
                with act.Fori(0, NB // (2 * PROJ)) as j:
                    act.wait_ge(h_ready[i], 1)
                    nc.scalar.activation(h_stage.rearrange("p (b f) -> p b f", f=F),
                                         h[:, bass.ds(j * (2 * PROJ), 2 * PROJ), :], ACT.Copy)\
                      .then_inc(h_staged[i], 1)
                    act.wait_ge(h_turned[i], j + 1)
                    nc.scalar.activation(h_t, banks(0, 2)[:, 0:PROJ * P], ACT.Copy)\
                      .then_inc(h_t_ready[i], 1)

            def root(k):
                act.wait_ge(root_in, k)
                nc.scalar.activation(rstd[:, :], rstd[:, :], ACT.Sqrt).then_inc(root_out, 1)

            def store_table(p, stage):
                act.wait_ge(table_ready[p], 1)
                act.dma_start(TABLE[p].rearrange("(b p) f -> p b f", p=P), stage).then_inc(table_out[p], 16)

            root(1)
            root(2)
            store_table(0, y_stage)
            store_table(1, y_stage)
            root(3)
            turn_h(0, acc64)
            store_table(2, kv_stage)
            p = 2
            act.wait_ge(turned[p], 1)
            nc.scalar.activation(onehot_t[0], turned_hot, ACT.Copy)\
              .then_inc(turned_read[p], 1)
            with act.Fori(0, ITERS) as it:
                for s in range(S):
                    act.wait_ge(exp_in[p], it * S + s + 1)
                    nc.scalar.activation(rows[s][:, :, KV:KV + HEADS],
                                         att[:, :].rearrange("p (t h) -> p t h", h=HEADS), ACT.Exp)\
                      .then_inc(exp_out[p], 1)
                    act.wait_ge(turned[p], it * S + s + 2)
                    nc.scalar.activation(onehot_t[(s + 1) % 2], turned_hot, ACT.Copy)\
                      .then_inc(turned_read[p], 1)

            root(4)
            root(5)
            store_table(3, y_stage)
            root(6)
            for i in range(2):
                turn_h(1 + i, aux)
                p = 4 + i
                store_table(p, g_stage)

                def score(n, s, it):
                    act.wait_ge(hot_ready[p], n + 1)
                    act.wait_ge(landed[p][s], it * (16 * T) + 16 * T)
                    for t in range(T):
                        last = nc.scalar.activation(scores[:, t, :], nothot[s % 2][:, t, :], ACT.Identity,
                                                    bias=rows_e[s][:, t, F:F + 1], scale=-BIG)
                    last.then_inc(scores_ready[p], 1)

                def invert(s):
                    nc.scalar.activation(hot_e[s % 2], nothot[s % 2], ACT.Copy, bias=1.0, scale=-1.0)\
                      .then_inc(turned_read[p], 1)

                def attend(n, s, it, first, more):
                    if more:
                        act.wait_ge(turned[p], n + 1)
                        score(n + 1, (s + 1) % S, it + (s + 1) // S)
                        if not first:
                            act.wait_ge(used[p], n)
                        invert((s + 1) % S)
                    act.wait_ge(nodes_ready[p], n + 1)
                    nc.scalar.activation(fade[s % 2][:, :], fade_in[:, :], ACT.Exp).then_inc(fade_out[p], 1)
                    act.wait_ge(exp_in[p], n + 1)
                    nc.scalar.activation(weight[:, :], edge_b[:, :], ACT.Exp).then_inc(exp_out[p], 1)

                score(0, 0, 0)
                invert(0)
                for s in range(S):
                    attend(s, s, 0, s == 0, True)
                if ITERS > 2:
                    with act.Fori(1, ITERS - 1) as it:
                        for s in range(S):
                            attend(it * S + s, s, it, False, True)
                for s in range(S):
                    attend((ITERS - 1) * S + s, s, ITERS - 1, False, s < S - 1)

        @block.tensor
        def _(pe):
            mm = nc.tensor.matmul
            for d in range(2):
                pe.wait_ge(counted, d + 1)
                mm(psum[:, d, 0:P], ones[:, :], counts[d][:, :], start=True, stop=True)
                mm(psum[:, d, P:2 * P], before[:, :], counts[d][:, :], start=True, stop=True)
                mm(psum[:, d, 2 * P:2 * P + 1], counts[d][:, :], ones[:, 0:1], start=True, stop=True)\
                    .then_inc(totals, 1)
                pe.wait_ge(columns, d + 1)
                mm(psum[:, d, 2 * P + 1:2 * P + 2], upto[:, :], col[1][:, :], start=True, stop=True)\
                    .then_inc(cum_cols, 1)
                pe.wait_ge(began_ready, d + 1)
                for j, c in enumerate(range(0, NC_, 512)):
                    w = min(512, NC_ - c)
                    if j or d:
                        pe.wait_ge(tables_read, d * len(range(0, NC_, 512)) + j)
                    mm(psum[:, 2, 0:w], real128[:, :], began[:, c:c + w], start=True, stop=True)
                    mm(psum[:, 3, 0:w], delta_wide[:, :], began[:, c:c + w], start=True, stop=True)\
                        .then_inc(tables_psum, 1)
            with pe.Fori(0, NBAT // 2) as n:
                for q in range(2):
                    pe.wait_ge(deg_hot, n * 2 + q + 1)
                    for k in range(CB):
                        for g in range(G):
                            last = mm(psum[:, 4 + q, k:k + 1], hot_bf[q][:, k * G + g, :], ones_bf[:, :],
                                      start=(g == 0), stop=(g == G - 1))
                    last.then_inc(deg_psum, 1)

            def linear(p):
                with pe.Fori(0, ITERS) as it:
                    for s in range(S):
                        q = s % 2
                        pe.wait_ge(hot_ready[p], it * S + s + 1)
                        pe.wait_ge(landed[p][s], it * (16 * T) + 16 * T)
                        pe.wait_ge(added[p][q], it * (CB * S // 2) + CB * (s // 2) + 1)
                        for k in range(CB):
                            for g in range(G):
                                last = mm(psum[:, 2 * q + k // 4, (k % 4) * F:(k % 4) * F + F], onehot[q][:, k * G + g, :],
                                          rows[s][:, k * G + g, 0:F], start=(g == 0), stop=(g == G - 1))
                            if k == CB // 2 - 1:
                                last.then_inc(summed[p], 1)
                            if k == CB - 1:
                                last.then_inc(used[p], 1)

            def project(i, w, width):
                with pe.Fori(0, NB // (2 * PROJ)) as j:
                    for k in range(PROJ):
                        if k == 0:
                            pe.wait_ge(h_staged[i], j + 1)
                        last = nc.tensor.transpose(banks(0, 2)[:, k * P:k * P + P],
                                                   h_stage[:, k * P:k * P + P], ident[:, :])
                    last.then_inc(h_turned[i], 1)
                    pe.wait_ge(h_t_ready[i], j + 1)
                    pe.wait_ge(proj_read[i], j * PROJ + 1)
                    for k in range(PROJ):
                        mm(psum[:, 2 + k, 0:width], h_t[:, k * P:k * P + P], w, start=True, stop=True)\
                            .then_inc(projected[i], 1)

            linear(0)
            linear(1)

            pe.wait_ge(weights_in, 16 * 17)
            project(0, w_qkv[:, :, :].rearrange("p a b -> p (a b)"), 6 * F)
            p = 2

            def turn(buf):
                for t in range(T):
                    last = nc.tensor.transpose(turned_hot[:, t, :], buf[:, t, :], ident_bf[:, :])
                last.then_inc(turned[p], 1)

            pe.wait_ge(hot_ready[p], 1)
            pe.wait_ge(proj_read[0], PROJ * (NB // (2 * PROJ)) + 1)
            turn(onehot_bf[0])
            with pe.Fori(0, ITERS) as it:
                for s in range(S):
                    q = s % 2
                    n = it * S + s
                    _, blocks = nc.values_load_multi_w_load_instructions(
                        chunk_int[BLOCK_ROW[1]:BLOCK_ROW[1] + 1, bass.ds(n * CB, CB)],
                        engines=PE_ONLY, min_val=0, max_val=NBLK,
                        skip_runtime_bounds_check_because="a count of blocks")
                    pe.wait_ge(turned_read[p], n + 1)
                    pe.wait_ge(spread[p], n + 1)
                    for t in range(T):
                        last = mm(psum[:, 4 + t // 8, (t % 8) * F:(t % 8) * F + F], onehot_t[q][:, t, :],
                                  aux[:, bass.ds(blocks[t // G], 1), :].rearrange("p o f -> p (o f)"),
                                  start=True, stop=True)
                    last.then_inc(nodes_ready[p], 1)
                    pe.wait_ge(hot_ready[p], n + 2)
                    turn(onehot_bf[1 - q])
                    pe.wait_ge(rows_ready[p], n + 1)
                    pe.wait_ge(added[p][0], n * CB + 1)
                    parts = (upper(rows[s][:, :, F:ROW]), upper(rest), last_part)
                    for k in range(CB):
                        for g in range(G):
                            for i, part in enumerate(parts):
                                last = mm(psum[:, 6 + k // 4, (k % 4) * MSG:(k % 4) * MSG + MSG],
                                          onehot_bf[q][:, k * G + g, :], part[:, k * G + g, :],
                                          start=(g == 0 and i == 0), stop=(g == G - 1 and i == 2))
                        if k == CB // 2 - 1:
                            last.then_inc(summed[p], 1)
                        if k == CB - 1:
                            last.then_inc(used[p], 1)

            linear(3)

            for i in range(2):
                p = 4 + i
                project(1 + i, w_gat[i][:, :, :].rearrange("p a b -> p (a b)"), 2 * F)
                pe.wait_ge(tabs_ready[i], 1)
                nc.tensor.transpose(psum[:, 0, 0:P], ad_tab[:, :], ident[:, :])
                nc.tensor.transpose(psum[:, 0, P:2 * P], self_tab[:, :], ident[:, :]).then_inc(tabs_turned[i], 1)
                pe.wait_ge(tabs_t_ready[i], 1)
                pieces = list(range(0, NC_, 512))
                assert len(pieces) <= 4
                for side in range(2):
                    for j, c in enumerate(pieces):
                        w = min(512, NC_ - c)
                        last = mm(psum[:, side * 4 + j, 0:w], tab_t[:, side, :], block_hot[:, c:c + w],
                                  start=True, stop=True)
                last.then_inc(spread_psum[i], 1)

                def turn_scores(n):
                    pe.wait_ge(scores_ready[p], n + 1)
                    for t in range(T):
                        last = nc.tensor.transpose(banks(0, 4)[:, t * P:t * P + P], scores[:, t, :], ident[:, :])
                    last.then_inc(turned[p], 1)

                def attend(n, s, more):
                    pe.wait_ge(nodes_ready[p], n + 1)
                    for t in range(T):
                        for i in range(3):
                            last = mm(psum[:, 4, 2 * t:2 * t + 2], hot_te[:, t, :],
                                      upper(node_pair[i][:, :, :])[:, t // G, :], start=(i == 0), stop=(i == 2))
                    last.then_inc(spread[p], 1)
                    if more:
                        turn_scores(n + 1)
                    pe.wait_ge(turned_read[p], n + 1)
                    pe.wait_ge(rows_ready[p], n + 1)
                    for k in range(CB):
                        for g in range(G):
                            last = mm(psum[:, 5 + k // 4, (k % 4) * 65:(k % 4) * 65 + 65],
                                      hot_e[s % 2][:, k * G + g, :], rows_e[s][:, k * G + g, :],
                                      start=(g == 0), stop=(g == G - 1))
                        if k == CB // 2 - 1:
                            last.then_inc(summed[p], 1)
                        if k == CB - 1:
                            last.then_inc(used[p], 1)

                turn_scores(0)
                if ITERS > 1:
                    with pe.Fori(0, ITERS - 1) as it:
                        for s in range(S):
                            attend(it * S + s, s, True)
                for s in range(S):
                    attend((ITERS - 1) * S + s, s, s < S - 1)

        @block.vector
        def _(dve):
            v = nc.vector

            def wide(a, shape):
                return a.to_broadcast(shape)

            dve.wait_ge(iotas, 1)
            v.tensor_tensor(ident[:, :], iota[:, :], col_no[:, :], ALU.is_equal)
            v.tensor_tensor(ident_bf[:, :], iota[:, :], col_no[:, :], ALU.is_equal)
            v.tensor_tensor(before[:, :], iota[:, :], col_no[:, :], ALU.is_gt)
            v.tensor_tensor(upto[:, :], iota[:, :], col_no[:, :], ALU.is_ge)
            v.tensor_scalar(real128[:, :], col_no[:, :], float(NBLK), float(P), ALU.is_lt, ALU.mult)
            v.tensor_scalar(half_up[:, :], iota[:, :], 0.5, None, ALU.add)
            dve.drain().then_inc(consts, 1)

            dve.wait_ge(edges_in, 32)
            v.tensor_scalar(block_int, dst32, 7, None, ALU.logical_shift_right)
            dve.drain()
            v.tensor_copy(dst_block, block_int).then_inc(keys_split, 1)
            dve.drain()
            v.tensor_scalar(block_int, src32, 7, None, ALU.logical_shift_right)
            v.memset(counts[0][:, :], 0.0)
            v.memset(counts[1][:, :], 0.0)
            dve.drain()
            v.tensor_copy(src_block, block_int)
            v.tensor_copy(dst_pairs[:, :, 0], src32)
            v.tensor_copy(dst_pairs[:, :, 1], dst32)
            v.tensor_copy(src_pairs[:, :, 0], dst32)
            v.tensor_copy(src_pairs[:, :, 1], src32)
            dve.drain().then_inc(pairs_made, 1)
            with dve.Fori(0, NBLK) as b:
                dve.drain()
                v.tensor_scalar(block_hit_bf, src_block, iota[:, bass.ds(b, 1)], 0.0, ALU.is_equal, ALU.add,
                                accum_out=counts[1][:, bass.ds(b, 1)])
            dve.drain()
            dve.wait_ge(dst_counted, 1)
            v.tensor_scalar(cumul[:, 1:NBLK + 1], cumul[:, 1:NBLK + 1], float(EP), 0.5, ALU.add, ALU.mult)
            dve.drain()
            v.tensor_tensor(counts[0][:, 0:NBLK], cumul[:, 1:NBLK + 1], cumul[:, 0:NBLK], ALU.subtract)
            dve.drain()

            for d in range(2):
                dve.drain().then_inc(counted, 1)
                dve.wait_ge(totals, d + 1)
                v.tensor_copy(col[0][:, :], psum[:, d, 2 * P:2 * P + 1])
                v.tensor_scalar(col_int[:, :], psum[:, d, 2 * P:2 * P + 1], float(CH - 1), None, ALU.add)
                dve.drain()
                v.tensor_scalar(col_int[:, :], col_int[:, :], CH.bit_length() - 1, None, ALU.logical_shift_right)
                dve.drain()
                v.tensor_copy(col[1][:, :], col_int[:, :])
                dve.drain()
                v.scalar_tensor_tensor(col[2][:, :], col[1][:, :], float(-CH), col[0][:, :], ALU.mult, ALU.add)\
                    .then_inc(columns, 1)
                dve.drain()
                if d:
                    dve.wait_ge(tables_psum, len(range(0, NC_, 512)))
                v.tensor_copy(delta_wide[:, :], wide(col[2][:, 0:1], [P, P]))
                dve.wait_ge(cum_cols, d + 1)
                v.tensor_copy(col[3][:, :], psum[:, d, 2 * P + 1:2 * P + 2])
                dve.drain()
                v.tensor_scalar(began, chunk_no, col[3][:, 0:1], None, ALU.is_ge)
                dve.drain()
                v.tensor_copy(small[3][:, 0:1], col[3][:, :]).then_inc(began_ready, 1)
                for j, c in enumerate(range(0, NC_, 512)):
                    w = min(512, NC_ - c)
                    dve.wait_ge(tables_psum, d * len(range(0, NC_, 512)) + j + 1)
                    v.tensor_copy(block128[d][:, c:c + w], psum[:, 2, 0:w])
                    r = BLOCK_ROW[d]
                    v.tensor_scalar(chunk_int[r:r + 1, c:c + w], psum[r:r + 1, 2, 0:w], 1.0 / P, None, ALU.mult)
                    r = OFFSET_ROW[d]
                    dve.drain()
                    v.scalar_tensor_tensor(running[r:r + 1, c:c + w], chunk_no[r:r + 1, c:c + w], float(CH),
                                           psum[r:r + 1, 3, 0:w], ALU.mult, ALU.add).then_inc(tables_read, 1)
                    dve.drain()
                    v.tensor_scalar(chunk_int[r:r + 1, c:c + w], running[r:r + 1, c:c + w], float(E), None, ALU.min)
                dve.drain().then_inc(offsets_ready, 1)

            v.memset(small[0][:, :], 0.0)
            v.tensor_copy(small[2][:, :], psum[:, 1, 0:P])
            dve.drain()
            v.tensor_tensor_scan(small[1][:, :], small[2][:, :], small[0][:, :], 0.0, ALU.add, ALU.add)
            dve.drain()
            v.scalar_tensor_tensor(small[1][:, :], small[1][:, :], -1.0, small[2][:, :], ALU.add, ALU.subtract)
            dve.drain()
            v.tensor_tensor(small[1][:, :], small[1][:, :], psum[:, 1, P:2 * P], ALU.add)
            dve.drain()
            for g, (lo, hi) in enumerate(SEGMENTS):
                part = slice(lo * SC, hi * SC)
                with dve.Fori(0, NBLK) as b:
                    v.tensor_scalar(block_hit[:, part], src_block[:, part], iota[:, bass.ds(b, 1)], None,
                                    ALU.is_equal)
                    dve.drain()
                    v.tensor_tensor_scan(running[:, part], block_hit[:, part], block_hit[:, part],
                                         small[1][:, bass.ds(b, 1)], ALU.add, ALU.bypass)
                    dve.drain()
                    v.copy_predicated(sorted_at[:, part], block_hit[:, part].bitcast(i32), running[:, part])
                    v.tensor_scalar(small[1][:, bass.ds(b, 1)], running[:, hi * SC - 1:hi * SC], 1.0, None,
                                    ALU.mult)
                    dve.drain()
                if hi == EP // SC:
                    v.memset(xr[:, :], 0.0).then_inc(x_region_free, 1)
                dve.drain().then_inc(places_ready, 1)

            for ahead in [a for p in LINEAR for a in added[p]] + [added[2][0], spread[2], *proj_read]:
                dve.sem_inc(ahead, 1)

            def load_blocks(direction, n):
                _, blocks = nc.values_load_multi_w_load_instructions(
                    chunk_int[BLOCK_ROW[direction]:BLOCK_ROW[direction] + 1, bass.ds(n * CB, CB)],
                    engines=DVE_ONLY, min_val=0, max_val=NBLK,
                    skip_runtime_bounds_check_because="a count of blocks")
                return blocks

            def keys_to_local(direction, n, drained=True):
                if drained:
                    dve.drain()
                v.tensor_tensor(local[:, :].rearrange("p (k g) -> p k g", g=G),
                                pairs[direction][:, bass.ds(n * CB, CB), :, 1],
                                wide(block128[direction][:, bass.ds(n * CB, CB)].unsqueeze(2), [P, CB, G]),
                                ALU.subtract)

            def compare(to, op):
                return v.tensor_tensor(to, wide(iota_bf[:, :].unsqueeze(1), [P, T, P]),
                                       wide(local[:, :].unsqueeze(2), [P, T, P]), op)

            def stage_index(p, s, n):
                v.tensor_scalar(index[s][:, :].rearrange("p (k g) -> p k g", g=G),
                                pairs[DIRECTION[p]][:, bass.ds(n * CB, CB), :, 0], 0, None, ALU.add)\
                    .then_inc(staged[p], 1)

            deg = dis_dst
            v.memset(deg[:, :], 0.0)

            def add_deg(n, q):
                blocks = load_blocks(0, n)
                for k in range(CB):
                    dve.drain()
                    if k == 0:
                        dve.wait_ge(deg_psum, n + 1)
                    v.tensor_tensor(deg[:, bass.ds(blocks[k], 1)], deg[:, bass.ds(blocks[k], 1)],
                                    psum[:, 4 + q, k:k + 1], ALU.add)

            def deg_hots(n, q):
                dve.drain()
                dve.wait_ge(loaded[0], n + 1)
                keys_to_local(0, n, False)
                dve.drain()
                compare(hot_bf[q], ALU.is_equal).then_inc(deg_hot, 1)

            dve.wait_ge(pairs_out, 48)
            deg_hots(0, 0)
            with dve.Fori(0, NBAT // 2) as i:
                for q in range(2):
                    if q == 0:
                        deg_hots(i * 2 + 1, 1)
                    add_deg(i * 2 + q, q)
                    if q == 1:
                        deg_hots(i * 2 + 2, 0)
            dve.drain()

            roots = [0]

            def reciprocal_root():
                roots[0] += 1
                dve.drain().then_inc(root_in, 1)
                dve.wait_ge(root_out, roots[0])
                v.reciprocal(rstd[:, :], rstd[:, :])
                dve.drain()

            def inverse_root(t):
                v.tensor_scalar(mean[:, :], t[:, :], 0.0, None, ALU.is_gt)
                v.tensor_scalar(rstd[:, :], t[:, :], 1.0, None, ALU.max)
                dve.drain()
                reciprocal_root()
                v.tensor_tensor(t[:, :], mean[:, :], rstd[:, :], ALU.mult)
                dve.drain()

            def norm_relu(to):
                v.tensor_reduce(mean[:, :], x, AX.X, ALU.add)
                dve.drain()
                v.tensor_scalar(mean[:, :], mean[:, :], 1.0 / F, None, ALU.mult)
                dve.drain()
                v.tensor_tensor(centered, x, wide(mean[:, :].unsqueeze(2), [P, NB, F]), ALU.subtract)
                dve.drain()
                v.tensor_tensor(squares, centered, centered, ALU.mult)
                dve.drain()
                v.tensor_reduce(rstd[:, :], squares, AX.X, ALU.add)
                dve.drain()
                v.tensor_scalar(rstd[:, :], rstd[:, :], 1.0 / F, 1e-5, ALU.mult, ALU.add)
                dve.drain()
                reciprocal_root()
                last = v.scalar_tensor_tensor(to, centered, 0.0, wide(rstd[:, :].unsqueeze(2), [P, NB, F]),
                                              ALU.max, ALU.mult)
                return last

            def scaled(to, a, per_node):
                return v.tensor_tensor(to, a, wide(per_node.unsqueeze(2), [P, NB, F]), ALU.mult)

            def add_to_x(scalar, a):
                v.scalar_tensor_tensor(x, a, scalar, x, ALU.mult, ALU.add)

            def all_pairs_in(p):
                dve.wait_ge(loaded[DIRECTION[p]], NBAT + S)

            def first_indices(p):
                all_pairs_in(p)
                for s in range(S):
                    stage_index(p, s, s)

            def linear(p):
                d = DIRECTION[p]
                first_indices(p)
                keys_to_local(d, 0)
                dve.drain()
                compare(onehot[0], ALU.is_equal).then_inc(hot_ready[p], 1)
                with dve.Fori(0, ITERS) as it:
                    for s in range(S):
                        q = s % 2
                        n = it * S + s
                        dve.drain()
                        keys_to_local(d, n + 1)
                        dve.drain()
                        compare(onehot[1 - q], ALU.is_equal).then_inc(hot_ready[p], 1)
                        blocks = load_blocks(d, n)
                        for k in range(CB):
                            dve.drain()
                            if k == 0:
                                dve.wait_ge(summed[p], n + 1)
                            if k == CB // 2:
                                dve.wait_ge(used[p], n + 1)
                            v.tensor_tensor(acc64[:, bass.ds(blocks[k], 1), :].rearrange("p o f -> p (o f)"),
                                            acc64[:, bass.ds(blocks[k], 1), :].rearrange("p o f -> p (o f)"),
                                            psum[:, 2 * q + k // 4, (k % 4) * F:(k % 4) * F + F], ALU.add).then_inc(added[p][q], 1)
                        stage_index(p, s, n + S)
                dve.drain()

            inverse_root(dis_dst)
            dve.wait_ge(x_in_sem, 32 if TAIL else 16)
            dve.wait_ge(weights_in, 16 * 17)
            norm_relu(acc64)
            dve.drain()
            add_to_x(alpha[:, 0:1], acc64)
            scaled(y_stage, acc64, dis_dst[:, :]).then_inc(table_ready[0], 1)
            dve.drain()
            v.memset(accr[:, :], 0.0)
            dve.drain()
            dve.wait_ge(table_out[0], 16)
            linear(0)
            scaled(acc64, acc64, dis_dst[:, :])
            dve.drain()
            add_to_x(alpha[:, 1:2], acc64)
            scaled(y_stage, acc64, dis_dst[:, :]).then_inc(table_ready[1], 1)
            dve.drain()
            v.memset(accr[:, :], 0.0)
            dve.drain()
            dve.wait_ge(table_out[1], 16)
            linear(1)
            scaled(acc64, acc64, dis_dst[:, :])
            dve.drain()
            add_to_x(alpha[:, 2:3], acc64)
            dve.drain()

            norm_relu(acc64)
            dve.drain().then_inc(h_ready[0], 1)
            with dve.Fori(0, NB // (2 * PROJ)) as j:
                for k in range(PROJ):
                    b2 = j * (2 * PROJ) + 2 * k
                    o = psum[:, 2 + k, 0:6 * F].rearrange("p (b f) -> p b f", b=2)
                    dve.wait_ge(projected[0], j * PROJ + k + 1)
                    v.tensor_scalar(aux[:, bass.ds(b2, 2), :], o[:, :, 0:F], 1.0, None, ALU.mult)
                    v.tensor_scalar(kv_stage[:, bass.ds(b2, 2), :], o[:, :, F:3 * F], 1.0, None, ALU.mult)\
                        .then_inc(proj_read[0], 1)
            dve.drain()
            v.memset(accr[:, :], 0.0).then_inc(table_ready[2], 1)
            dve.wait_ge(table_out[2], 16)
            p = 2
            for s in range(S):
                v.memset(rows[s][:, :, ROW - 1:ROW], 1.0)
            first_indices(p)
            keys_to_local(1, 0)
            dve.drain()
            compare(onehot_bf[0], ALU.is_equal).then_inc(hot_ready[p], 1)

            def add_attention(n):
                blocks = load_blocks(1, n)
                for k in range(CB):
                    dve.drain()
                    if k == 0:
                        dve.wait_ge(summed[p], n + 1)
                    if k == CB // 2:
                        dve.wait_ge(used[p], n + 1)
                    a = acc69[:, bass.ds(blocks[k], 1), :].rearrange("p o f -> p (o f)")
                    v.tensor_tensor(a, a, psum[:, 6 + k // 4, (k % 4) * MSG:(k % 4) * MSG + MSG], ALU.add)\
                        .then_inc(added[p][0], 1)

            with dve.Fori(0, ITERS) as it:
                for s in range(S):
                    q = s % 2
                    n = it * S + s
                    dve.wait_ge(landed[p][s], it * (16 * T) + 16 * T)
                    dve.wait_ge(nodes_ready[p], n + 1)
                    v.tensor_tensor(products, rows[s][:, :, 0:F],
                                    banks(4, 2).rearrange("p (t f) -> p t f", f=F), ALU.mult)\
                        .then_inc(spread[p], 1)
                    dve.drain()
                    v.tensor_reduce(att[:, :], products.rearrange("p t (h d) -> p (t h) d", d=DH), AX.X, ALU.add)
                    dve.drain()
                    v.tensor_scalar(att[:, :], att[:, :], -10.0, 10.0, ALU.max, ALU.min).then_inc(exp_in[p], 1)
                    keys_to_local(1, n + 1)
                    dve.drain()
                    compare(onehot_bf[1 - q], ALU.is_equal).then_inc(hot_ready[p], 1)
                    dve.wait_ge(exp_out[p], n + 1)
                    vv = rows[s][:, :, F:KV].rearrange("p t (h d) -> p t h d", d=DH)
                    v.tensor_tensor(vv, vv, wide(rows[s][:, :, KV:KV + HEADS].unsqueeze(3), [P, T, HEADS, DH]),
                                    ALU.mult)
                    dve.drain()
                    msg = rows[s][:, :, F:ROW]
                    v.tensor_tensor(rest, msg, upper(msg), ALU.subtract)
                    dve.drain()
                    v.tensor_tensor(last_part, rest, upper(rest), ALU.subtract).then_inc(rows_ready[p], 1)
                    add_attention(n)
                    stage_index(p, s, n + S)
            dve.drain()

            v.tensor_copy(dis_src[:, :], acc69[:, :, F + HEADS])
            den = acc69[:, :, F:F + HEADS]
            v.tensor_scalar(den, den, 1e-8, None, ALU.add)
            dve.drain()
            v.reciprocal(den, den)
            dve.drain()
            num = acc69[:, :, 0:F].rearrange("p b (h d) -> p b h d", d=DH)
            v.tensor_tensor(num, num, wide(den.unsqueeze(3), [P, NB, HEADS, DH]), ALU.mult)
            dve.drain()
            v.tensor_tensor(x, x, acc69[:, :, 0:F], ALU.add)
            inverse_root(dis_src)

            norm_relu(acc64)
            dve.drain()
            scaled(y_stage, acc64, dis_src[:, :]).then_inc(table_ready[3], 1)
            dve.drain()
            v.memset(accr[:, :], 0.0)
            dve.drain()
            dve.wait_ge(table_out[3], 16)
            linear(3)
            scaled(acc64, acc64, dis_src[:, :])
            dve.drain()
            v.tensor_tensor(x, x, acc64, ALU.add)
            dve.drain()

            def gat(i, a_src, a_dst):
                p = 4 + i
                dve.drain().then_inc(h_ready[1 + i], 1)
                with dve.Fori(0, NB // (2 * PROJ)) as j:
                    for k in range(PROJ):
                        b2 = j * (2 * PROJ) + 2 * k
                        o = psum[:, 2 + k, 0:2 * F].rearrange("p (b f) -> p b f", b=2)
                        dve.wait_ge(projected[1 + i], j * PROJ + k + 1)
                        v.tensor_scalar(g_stage[:, bass.ds(b2, 2), 0:F], o, 1.0, None, ALU.mult)\
                            .then_inc(proj_read[1 + i], 1)
                dve.drain()
                g = g_stage[:, :, 0:F]
                v.memset(ad_tab[:, :], 0.0)
                v.memset(self_tab[:, :], 0.0)
                v.tensor_tensor(g_times, g, wide(a_src[:, :].unsqueeze(1), [P, NB, F]), ALU.mult)
                dve.drain()
                v.tensor_reduce(mean[:, :], g_times, AX.X, ALU.add)
                dve.drain()
                v.tensor_tensor(g_times, g, wide(a_dst[:, :].unsqueeze(1), [P, NB, F]), ALU.mult)
                dve.drain()
                v.tensor_reduce(ad_tab[:, 0:NB], g_times, AX.X, ALU.add)
                v.tensor_copy(g_stage[:, :, F], mean[:, :])
                dve.drain()
                v.tensor_tensor(rstd[:, :], mean[:, :], ad_tab[:, 0:NB], ALU.add)
                dve.drain()
                v.scalar_tensor_tensor(self_tab[:, 0:NB], rstd[:, :], 0.2, rstd[:, :], ALU.mult, ALU.max)
                v.tensor_copy(acc65[:, :, 0:F], g)
                v.memset(acc65[:, :, F:F + 1], 1.0)
                dve.drain().then_inc(table_ready[p], 1)
                v.tensor_scalar(block_hot, block128[0][:, :], 1.0 / P, col_no[:, 0:1], ALU.mult, ALU.is_equal)
                v.memset(fresh[:, 0:1], -BIG)
                v.tensor_tensor(fresh[:, 1:NC_], block128[0][:, 1:NC_], block128[0][:, 0:NC_ - 1], ALU.not_equal)
                dve.drain()
                v.tensor_scalar(fresh[:, 1:NC_], fresh[:, 1:NC_], -BIG, None, ALU.mult).then_inc(tabs_ready[i], 1)
                dve.wait_ge(tabs_turned[i], 1)
                v.tensor_copy(tab_t[:, :, :], psum[:, 0, 0:2 * P].rearrange("p (a b) -> p a b", a=2))\
                    .then_inc(tabs_t_ready[i], 1)
                dve.wait_ge(spread_psum[i], 1)
                v.tensor_copy(ad_chunk, banks(0, 4)[:, 0:NC_])
                v.tensor_copy(self_chunk, banks(4, 4)[:, 0:NC_])
                dve.wait_ge(table_out[p], 16)
                dve.drain()

                first_indices(p)
                v.memset(peak[1][:, :], -BIG)
                for n in range(2):
                    keys_to_local(0, n)
                    dve.drain()
                    compare(nothot[n], ALU.not_equal).then_inc(hot_ready[p], 1)

                def add_chunks(n, q):
                    blocks = load_blocks(0, n)
                    dve.drain()
                    dve.wait_ge(fade_out[p], n + 1)
                    for k in range(CB):
                        if k:
                            dve.drain()
                        if k == 0:
                            dve.wait_ge(summed[p], n + 1)
                        if k == CB // 2:
                            dve.wait_ge(used[p], n + 1)
                        a = acc65[:, bass.ds(blocks[k], 1), :].rearrange("p o f -> p (o f)")
                        v.scalar_tensor_tensor(a, a, fade[q][:, k:k + 1],
                                               psum[:, 5 + k // 4, (k % 4) * 65:(k % 4) * 65 + 65],
                                               ALU.mult, ALU.add)

                def attend(n, s, it, first):
                    q = s % 2
                    dve.wait_ge(turned[p], n + 1)
                    v.tensor_reduce(chunk_max[:, :], banks(0, 4).rearrange("p (k e) -> p k e", k=CB),
                                    AX.X, ALU.max)
                    v.tensor_scalar(hot_te, banks(0, 4).rearrange("p (t e) -> p t e", t=T), -BIG / 2, None,
                                    ALU.is_gt)
                    ad_now = ad_chunk[:, bass.ds(n * CB, CB)]
                    self_now = self_chunk[:, bass.ds(n * CB, CB)]
                    fresh_now = fresh[:, bass.ds(n * CB, CB)]
                    dve.drain()
                    v.tensor_tensor(leak[:, :], chunk_max[:, :], ad_now, ALU.add)
                    v.tensor_scalar(node_pair[0][:, :, 0], ad_now, 1.0, None, ALU.mult)
                    v.tensor_copy(peak[q][:, 0:1], peak[1 - q][:, CB:CB + 1])
                    dve.drain()
                    v.scalar_tensor_tensor(leak[:, :], leak[:, :], 0.2, leak[:, :], ALU.mult, ALU.max)
                    dve.drain()
                    v.tensor_tensor(leak[:, :], leak[:, :], self_now, ALU.max)
                    dve.drain()
                    v.tensor_tensor_scan(peak[q][:, 1:CB + 1], fresh_now, leak[:, :], peak[q][:, 0:1],
                                         ALU.add, ALU.max)
                    dve.drain()
                    v.tensor_copy(node_pair[0][:, :, 1], peak[q][:, 1:CB + 1])
                    v.tensor_tensor(fade_in[:, :], peak[q][:, 0:CB], fresh_now, ALU.add)
                    dve.drain()
                    v.tensor_tensor(node_pair[1][:, :, :], node_pair[0][:, :, :], upper(node_pair[0][:, :, :]),
                                    ALU.subtract)
                    v.tensor_tensor(fade_in[:, :], fade_in[:, :], self_now, ALU.max)
                    dve.drain()
                    v.tensor_tensor(node_pair[2][:, :, :], node_pair[1][:, :, :], upper(node_pair[1][:, :, :]),
                                    ALU.subtract)
                    v.tensor_tensor(fade_in[:, :], fade_in[:, :], peak[q][:, 1:CB + 1], ALU.subtract)
                    dve.drain().then_inc(nodes_ready[p], 1)
                    keys_to_local(0, n + 2, False)
                    dve.drain()
                    dve.wait_ge(turned_read[p], n + 1)
                    compare(nothot[q], ALU.not_equal).then_inc(hot_ready[p], 1)
                    dve.wait_ge(spread[p], n + 1)
                    pair = psum[:, 4, 0:2 * T].rearrange("p (t c) -> p t c", c=2)
                    v.tensor_tensor(edge_a[:, :], rows_e[s][:, :, F], pair[:, :, 0], ALU.add)
                    dve.drain()
                    v.scalar_tensor_tensor(edge_a[:, :], edge_a[:, :], 0.2, edge_a[:, :], ALU.mult, ALU.max)
                    dve.drain()
                    v.tensor_tensor(edge_a[:, :], edge_a[:, :], pair[:, :, 1], ALU.subtract)
                    dve.drain()
                    v.tensor_scalar(edge_b[:, :], edge_a[:, :], 0.0, None, ALU.min).then_inc(exp_in[p], 1)
                    if not first:
                        add_chunks(n - 1, 1 - q)
                        stage_index(p, (s - 1) % S, n - 1 + S)
                    dve.wait_ge(exp_out[p], n + 1)
                    v.tensor_tensor(rows_e[s][:, :, 0:F], rows_e[s][:, :, 0:F],
                                    wide(weight[:, :].unsqueeze(2), [P, T, F]), ALU.mult)
                    v.tensor_copy(rows_e[s][:, :, F], weight[:, :])
                    dve.drain().then_inc(rows_ready[p], 1)

                for s in range(S):
                    attend(s, s, 0, s == 0)
                if ITERS > 2:
                    with dve.Fori(1, ITERS - 1) as it:
                        for s in range(S):
                            attend(it * S + s, s, it, False)
                for s in range(S):
                    attend((ITERS - 1) * S + s, s, ITERS - 1, False)
                add_chunks(NBAT - 1, (S - 1) % 2)
                dve.drain()
                den = acc65[:, :, F]
                v.tensor_scalar(mean[:, :], den, 1e-16, None, ALU.add)
                dve.drain()
                v.reciprocal(mean[:, :], mean[:, :])
                dve.drain()
                scaled(aux, acc65[:, :, 0:F], mean[:, :])
                dve.drain()

            norm_relu(aux)
            dve.drain()
            gat(0, vecs[0], vecs[1])
            v.tensor_tensor(aux, aux, wide(vecs[2][:, :].unsqueeze(1), [P, NB, F]), ALU.add)
            dve.drain()
            v.tensor_scalar(aux, aux, 0.0, None, ALU.max)
            dve.drain()
            gat(1, vecs[3], vecs[4])
            v.tensor_tensor(x, x, wide(vecs[5][:, :].unsqueeze(1), [P, NB, F]), ALU.add)
            dve.drain()
            v.tensor_tensor(x, x, aux, ALU.add).then_inc(out_ready, 1)


_INS = ['x', 'src', 'dst', 'L0_gnn_alpha', 'L1_gnn_Wq', 'L1_gnn_Wk', 'L1_gnn_Wv', 'L3_gnn_W1', 'L3_gnn_a_src1',
        'L3_gnn_a_dst1', 'L3_gnn_b1', 'L3_gnn_W2', 'L3_gnn_a_src2', 'L3_gnn_a_dst2', 'L3_gnn_b2']


def kernel(**inputs):
    import numpy as _np
    import concourse.bacc as _bacc
    from concourse.bass_utils import run_bass_kernel_spmd as _run

    nc = _bacc.Bacc("TRN2", target_bir_lowering=False, num_devices=1)
    arrays, args = {}, []
    for name in _INS:
        a = _np.ascontiguousarray(inputs[name])
        arrays[f"in_{name}_dram"] = a
        args.append(nc.dram_tensor(f"in_{name}_dram", a.shape, mybir.dt.from_np(a.dtype), kind="ExternalInput").ap())
    out = nc.dram_tensor("out_0_dram", arrays["in_x_dram"].shape, f32, kind="ExternalOutput").ap()
    gnn_kernel(nc, *args, out)
    r = _run(nc, [arrays], core_ids=[0])
    return r.results[0]["out_0_dram"]
```

```python
from contextlib import ExitStack

import concourse.bass as bass
from concourse import mybir

P = 128
G = 2
CH = G * P
CB = 8
T = CB * G
S = 4
F = 64
HEADS = 4
DH = F // HEADS
KV = 2 * F
ROW = 133
BIG = 1.0e30
NO_NODE = 20000
PROJ = 5

f32 = mybir.dt.float32
bf16 = mybir.dt.bfloat16
i32 = mybir.dt.int32
u32 = mybir.dt.uint32
i16 = mybir.dt.int16
ALU = mybir.AluOpType
ACT = mybir.ActivationFunctionType
AX = mybir.AxisListType
DVE_ONLY = (mybir.EngineType.DVE,)
PE_ONLY = (mybir.EngineType.PE,)
SP_ONLY = (mybir.EngineType.SP,)


def gnn_kernel(nc, x_in, src_in, dst_in, alpha_in, wq_in, wk_in, wv_in,
               w1_in, as1_in, ad1_in, b1_in, w2_in, as2_in, ad2_in, b2_in, out):
    N = x_in.shape[0]
    E = src_in.shape[0]
    EP = E // P
    assert EP * P == E and N < 16384
    NBLK = -(-N // P)
    FULL = N // P
    TAIL = N - FULL * P
    NB = 2 * PROJ * (-(-(NBLK + 1) // (2 * PROJ)))
    assert NB <= P and NB * P < 32768
    steps = NB // (2 * PROJ)
    HALVES = [(lo, hi) for lo, hi in ((0, -(-steps // 2)), (-(-steps // 2), steps)) if lo < hi]
    HB = [slice(lo * 2 * PROJ, hi * 2 * PROJ) for lo, hi in HALVES]
    NH = len(HALVES)
    NCH = -(-(E + NBLK * (CH - 1)) // CH)
    NBAT = -(-NCH // CB)
    NBAT = S * (-(-NBAT // S))
    NC_ = (NBAT + S) * CB
    ITERS = NBAT // S
    SC = next(d for d in (25, 5, 1) if EP % d == 0)
    SC0 = -(-SC // 2)
    SCH = (SC0, SC - SC0)
    units = EP // SC
    cuts = sorted({0, *(-(-units * part // 500) for part in (24, 60, 132, 308)), units})
    SEGMENTS = list(zip(cuts, cuts[1:]))
    SEG = SC * max(hi - lo for lo, hi in SEGMENTS)
    STAGED_LO, STAGED_HI = cuts[1], max(cuts[1], units * 4 // 5)
    COUNTED_BY_DVE = 3 * NBLK // 5 + 1

    y_table = nc.dram_tensor("y_table", (NB * P, F), f32).ap()
    kv_table = nc.dram_tensor("kv_table", (NB * P, KV), f32).ap()
    g_table = nc.dram_tensor("g_table", (NB * P, F + 1), f32).ap()
    by_dst = nc.dram_tensor("by_dst", (E + CH, 2), i16).ap()
    by_src = nc.dram_tensor("by_src", (E + CH, 2), i16).ap()

    ctx = ExitStack()
    with ctx:
        def sb(name, shape, dt):
            return ctx.enter_context(nc.sbuf_tensor(name, shape, dt))

        def sem(name):
            return ctx.enter_context(nc.semaphore(name))

        xr = sb("xr", [P, NB * F], f32)
        accr = sb("accr", [P, max(NB * (F + HEADS + 1), 2 * EP)], f32)
        auxr = sb("auxr", [P, max(NB * F, 3 * NC_, 2 * EP)], f32)
        ROWS = S * T * ROW
        work = sb("work", [P, ROWS + 4 * T * P], f32)

        def view(region, at, shape, dt=f32):
            n = 1
            for s in shape:
                n *= s
            size = n * (2 if dt in (bf16, i16) else 4)
            v = region[:, at:at + -(-size // 4)]
            if dt != f32:
                v = v.bitcast(dt)
            v = v[:, 0:n]
            if len(shape) == 2:
                v = v.rearrange("p (a b) -> p a b", b=shape[1])
            if len(shape) == 3:
                v = v.rearrange("p (a b c) -> p a b c", b=shape[1], c=shape[2])
            return v

        x = view(xr, 0, [NB, F])
        acc64 = view(accr, 0, [NB, F])
        acc69 = view(accr, 0, [NB, F + HEADS + 1])
        acc65 = view(accr, 0, [NB, F + 1])
        aux = view(auxr, 0, [NB, F])
        src32 = view(xr, 0, [EP], i32)
        dst32 = view(xr, EP, [EP], i32)
        src_block = view(accr, 0, [EP], bf16)
        block_hit = [view(accr, -(-EP // 2) + i * SEG, [SEG]) for i in range(2)]
        assert -(-EP // 2) + 2 * SEG <= accr.shape[1]
        block_hit_bf = view(accr, EP, [EP], bf16)
        block_int = view(accr, EP, [EP], i32)
        sorted_at = view(auxr, 0, [EP])
        src_pairs = view(auxr, EP, [EP, 2], i16)
        dst_block = view(work, 0, [EP])
        dst_pairs = view(work, EP, [EP, 2], i16)
        sign_out = view(work, 2 * EP, [EP])
        running = [view(work, 3 * EP, [EP]), view(work, EP, [EP])]
        AT = 4 * EP
        began = view(work, AT, [NC_])
        chunk_no = view(work, AT + NC_, [NC_])
        assert AT + 2 * NC_ <= ROWS + 4 * T * P
        centered = view(work, 0, [NB, F])
        squares = view(work, NB * F, [NB, F])
        y_stage = view(work, 0, [NB, F])
        kv_stage = view(work, 0, [NB, KV])
        g_stage = view(work, 0, [NB, F + 1])
        ROWS_E = S * T * (F + 1)
        BESIDE = max(NB * (F + 1), ROWS_E)
        block_hot = view(work, BESIDE, [NC_])
        BESIDE = max(NB * KV, BESIDE + NC_)
        h_t = view(work, BESIDE, [PROJ * P])
        tab_t = view(work, BESIDE + PROJ * P, [2, P])
        h_stage = view(work, BESIDE + PROJ * P + 2 * P, [PROJ * P])
        rows = [view(work, s * T * ROW, [T, ROW]) for s in range(S)]
        hot = [view(work, ROWS + i * T * P, [T, P]) for i in range(4)]
        hot_bf = [view(work, ROWS + i * T * P, [T, P], bf16) for i in range(2)]
        onehot = hot[0:2]
        onehot_bf = [view(work, ROWS + i * (T * P // 2), [T, P], bf16) for i in range(4)]
        onehot_t = view(work, ROWS + 2 * T * P, [T, P])
        MSG = F + HEADS + 1
        rest = view(work, ROWS + 3 * T * P, [T, MSG])
        last_part = view(work, ROWS + 3 * T * P + T * MSG, [T, MSG], bf16)
        rows_e = [view(work, s * T * (F + 1), [T, F + 1]) for s in range(S)]
        nothot = [view(work, ROWS_E + i * (T * P // 2), [T, P], bf16) for i in range(2)]
        scores = view(work, ROWS_E + T * P, [T, P])
        hot_e = [view(work, ROWS_E + (2 + i) * T * P, [T, P]) for i in range(2)]
        hot_te = view(work, ROWS_E + 4 * T * P, [T, P], bf16)
        assert ROWS_E + 5 * T * P <= ROWS + 4 * T * P

        def upper(a):
            names = "abcd"[:len(a.shape) - 1]
            outer, inner = " ".join(names[:-1]), names[-1]
            return a.bitcast(bf16).rearrange(f"p {outer} ({inner} w) -> p {outer} {inner} w", w=2)[..., 1]

        ad_chunk = view(auxr, 0, [NC_])
        self_chunk = view(auxr, NC_, [NC_])
        fresh = view(auxr, 2 * NC_, [NC_])

        pairs = [sb(f"pairs_{d}", [P, NC_, G, 2], i16) for d in ("by_dst", "by_src")]
        block128 = [sb(f"block128_{d}", [P, NC_], f32) for d in ("by_dst", "by_src")]
        chunk_int = sb("chunk_int", [P, NC_], i32)
        iota = sb("iota", [P, P], f32)
        ident = sb("ident", [P, P], f32)
        ident_bf = sb("ident_bf", [P, P], bf16)
        col_no = sb("col_no", [P, P], f32)
        before = sb("before", [P, P], f32)
        upto = sb("upto", [P, P], f32)
        ones = sb("ones", [P, P], f32)
        ones_bf = sb("ones_bf", [P, 1], bf16)
        half_up = sb("half_up", [P, P], f32)
        real128 = sb("real128", [P, P], f32)
        counts = [sb(f"counts_{d}", [P, P], f32) for d in ("by_dst", "by_src")]
        cumul = sb("cumul", [P, P + 1], f32)
        cumul_src = sb("cumul_src", [P, P + 1], f32)
        small = [sb(f"small{i}", [P, P], f32) for i in range(4)]
        col = [sb(f"col{i}", [P, 1], f32) for i in range(4)]
        col_int = sb("col_int", [P, 1], i32)
        delta_wide = sb("delta_wide", [P, P], f32)
        no_edge = sb("no_edge", [P, G, 2], i16)
        at_stage = [sb(f"at_stage{i}", [P, SC], i32) for i in range(2)]
        pair_stage = [sb(f"pair_stage{i}", [P, SC, 2], i16) for i in range(2)]
        index = [sb(f"index{s}", [P, T], i32) for s in range(S)]
        local = sb("local", [P, T], bf16)
        iota_bf = sb("iota_bf", [P, P], bf16)
        dis_dst = sb("dis_dst", [P, NB], f32)
        dis_src = sb("dis_src", [P, NB], f32)
        mean = sb("mean", [P, NB], f32)
        rstd = sb("rstd", [P, NB], f32)
        alpha = sb("alpha", [P, 3], f32)
        vecs = [sb(n, [P, F], f32) for n in ("as1", "ad1", "b1", "as2", "ad2", "b2")]
        w_qkv = sb("w_qkv", [P, 2, 3 * F], f32)
        w_gat = [sb(f"w_gat{i}", [P, 2, F + 2], f32) for i in range(2)]
        att = sb("att", [P, T * HEADS], f32)
        peak = [sb(f"peak{i}", [P, CB + 1], f32) for i in range(2)]
        chunk_max = sb("chunk_max", [P, CB], f32)
        leak = sb("leak", [P, CB], f32)
        fade_in = sb("fade_in", [P, CB], f32)
        fade = [sb(f"fade{i}", [P, CB], f32) for i in range(2)]
        node_pair = [sb(f"node_pair{i}", [P, CB, 2], f32) for i in range(3)]
        edge_a = sb("edge_a", [P, T], f32)
        edge_b = sb("edge_b", [P, T], f32)
        weight = sb("weight", [P, T], f32)
        ad_tab = sb("ad_tab", [P, P], f32)
        self_tab = sb("self_tab", [P, P], f32)

        psum = ctx.enter_context(nc.psum_tensor("psum", [P, 8, 512], f32))

        def banks(a, n):
            return psum[:, a:a + n, :].rearrange("p a b -> p (a b)")

        turned_hot = banks(0, 2).bitcast(bf16).rearrange("p (t n) -> p t n", n=P)

        edges_in = sem("edges_in")
        weights_in = sem("weights_in")
        iotas = sem("iotas")
        consts = sem("consts")
        keys_split = sem("keys_split")
        pairs_made = sem("pairs_made")
        pairs_out = sem("pairs_out")
        act_counted = sem("act_counted")
        counted = sem("counted")
        totals = sem("totals")
        columns = sem("columns")
        cum_cols = sem("cum_cols")
        began_ready = sem("began_ready")
        tables_psum = sem("tables_psum")
        tables_read = sem("tables_read")
        offsets_ready = sem("offsets_ready")
        places_ready = sem("places_ready")
        staged_pairs = sem("staged_pairs")
        staged_by_act = sem("staged_by_act")
        scattered = [sem(f"scattered{i}") for i in range(2)]
        started = sem("started")
        pairs_in = [sem(f"pairs_in{q}") for q in range(2)]
        loaded = [sem(f"loaded_{d}") for d in ("by_dst", "by_src")]
        x_in_sem = sem("x_in_sem")
        x_region_free = sem("x_region_free")
        deg_hot = sem("deg_hot")
        deg_psum = sem("deg_psum")
        table_ready = [sem(f"table_ready{p}") for p in range(6)]
        table_out = [sem(f"table_out{p}") for p in range(6)]
        h_ready = [sem(f"h_ready{i}") for i in range(3)]
        h_staged = [sem(f"h_staged{i}") for i in range(3)]
        h_turned = [sem(f"h_turned{i}") for i in range(3)]
        h_t_ready = [sem(f"h_t_ready{i}") for i in range(3)]
        projected = [sem(f"projected{i}") for i in range(3)]
        proj_read = [sem(f"proj_read{i}") for i in range(3)]
        tabs_ready = [sem(f"tabs_ready{i}") for i in range(2)]
        tabs_turned = [sem(f"tabs_turned{i}") for i in range(2)]
        tabs_t_ready = [sem(f"tabs_t_ready{i}") for i in range(2)]
        spread_psum = [sem(f"spread_psum{i}") for i in range(2)]
        centered_ready = sem("centered_ready")
        squared = sem("squared")
        root_in = sem("root_in")
        root_out = sem("root_out")
        out_ready = sem("out_ready")
        out_done = sem("out_done")
        LINEAR = (0, 1, 3)
        TURNING = (2, 4, 5)

        def sems(name, passes=range(6)):
            return {p: sem(f"{name}{p}") for p in passes}

        staged = sems("staged")
        landed = [[sem(f"landed{p}_{s}") for s in range(S)] for p in range(6)]
        used = sems("used")
        summed = sems("summed")
        hot_ready = sems("hot_ready")
        added = {p: [sem(f"added{p}_{q}") for q in range(2 if p in LINEAR else 1)] for p in range(6)}
        turned = sems("turned", TURNING)
        turned_read = sems("turned_read", TURNING)
        nodes_ready = sems("nodes_ready", TURNING)
        spread = sems("spread", TURNING)
        exp_in = sems("exp_in", TURNING)
        exp_out = sems("exp_out", TURNING)
        rows_ready = sems("rows_ready", TURNING)
        fade_out = sems("fade_out", TURNING[1:])
        scores_ready = sems("scores_ready", TURNING[1:])

        DIRECTION = (0, 0, 1, 1, 0, 0)
        TABLE = (y_table, y_table, kv_table, y_table, g_table, g_table)
        WIDTH = (F, F, KV, F, F + 1, F + 1)
        BLOCK_ROW = (0, 32)
        OFFSET_ROW = (64, 96)

        block = ctx.enter_context(nc.Block())

        @block.sync
        def _(sp):
            sp.dma_start(src32, src_in.rearrange("(p t) -> p t", t=EP)).then_inc(edges_in, 16)
            sp.dma_start(dst32, dst_in.rearrange("(p t) -> p t", t=EP)).then_inc(edges_in, 16)
            sp.dma_start(alpha[:, :], alpha_in.rearrange("(a n) -> a n", a=1).to_broadcast([P, 3]))\
              .then_inc(weights_in, 16)
            for v, a in zip(vecs, (as1_in, ad1_in, b1_in, as2_in, ad2_in, b2_in)):
                sp.dma_start(v[:, :], a.rearrange("(a n) -> a n", a=1).to_broadcast([P, F]))\
                  .then_inc(weights_in, 16)
            sp.wait_ge(iotas, 1)
            for half in range(2):
                part = slice(half * F, half * F + F)
                for k, w in enumerate((wq_in, wk_in, wv_in)):
                    sp.dma_start(w_qkv[part, half, k * F:k * F + F], w).then_inc(weights_in, 16)
                sp.dma_start(w_gat[0][part, half, 0:F], w1_in).then_inc(weights_in, 16)
                sp.dma_start(w_gat[1][part, half, 0:F], w2_in).then_inc(weights_in, 16)
            sp.wait_ge(pairs_made, 1)
            sp.dma_start(by_dst[0:E, :].rearrange("(p t) c -> p t c", t=EP), dst_pairs)\
              .then_inc(pairs_out, 16)
            for table in (by_dst, by_src):
                sp.dma_start(table[E:E + CH, :].rearrange("(p g) c -> p g c", g=G), no_edge[:, :, :])\
                  .then_inc(pairs_out, 16)
            def load_chunks(direction, table):
                before_this = direction * (NBAT + S) // 2 * (16 * CB)

                def load(n, q):
                    for k in range(CB):
                        at = sp.value_load(
                            chunk_int[OFFSET_ROW[direction]:OFFSET_ROW[direction] + 1,
                                      bass.ds(n * CB + k, 1)], min_val=0, max_val=E)
                        sp.dma_start(
                            pairs[direction][:, bass.ds(n * CB + k, 1), :, :].rearrange("p o g c -> p (o g c)"),
                            table[bass.ds(at, CH), :].rearrange("(p g) c -> p (g c)", g=G))\
                          .then_inc(pairs_in[q], 16)

                def arrived(i, q):
                    sp.wait_ge(pairs_in[q], i * (16 * CB) + (16 * CB + before_this))
                    sp.sem_inc(loaded[direction], 1)

                load(0, 0)
                with sp.Fori(0, (NBAT + S) // 2 - 1) as i:
                    load(i * 2 + 1, 1)
                    arrived(i, 0)
                    load(i * 2 + 2, 0)
                    arrived(i, 1)
                load(NBAT + S - 1, 1)
                for q in range(2):
                    arrived((NBAT + S) // 2 - 1, q)

            def store_table(p, stage):
                for h in range(NH):
                    sp.wait_ge(table_ready[p], h + 1)
                    sp.dma_start(TABLE[p].rearrange("(p b) f -> p b f", b=NB)[:, HB[h], :], stage[:, HB[h], :])\
                      .then_inc(table_out[p], 16)

            sp.wait_ge(offsets_ready, 2)
            sp.wait_ge(pairs_out, 48)
            load_chunks(0, by_dst)
            sp.wait_ge(x_region_free, 1)
            sp.dma_start(x[:, 0:FULL, :], x_in[0:FULL * P, :].rearrange("(b p) f -> p b f", p=P))\
              .then_inc(x_in_sem, 16)
            if TAIL:
                sp.dma_start(x[0:TAIL, FULL, :], x_in[FULL * P:N, :]).then_inc(x_in_sem, 16)
            store_table(0, y_stage)
            for i in range(2):
                sp.wait_ge(scattered[i], 16 * SCH[i] * (EP // SC))
            load_chunks(1, by_src)

            store_table(1, y_stage)
            store_table(2, kv_stage)
            store_table(3, y_stage)
            store_table(4, g_stage)
            store_table(5, g_stage)

            stores = 0
            for h in range(NH):
                sp.wait_ge(out_ready, h + 1)
                lo, hi = HB[h].start, min(HB[h].stop, FULL)
                if lo < hi:
                    sp.dma_start(out[lo * P:hi * P, :].rearrange("(b p) f -> p b f", p=P), x[:, lo:hi, :])\
                      .then_inc(out_done, 16)
                    stores += 1
                if TAIL and HB[h].start <= FULL < HB[h].stop:
                    sp.dma_start(out[FULL * P:N, :], x[0:TAIL, FULL, :]).then_inc(out_done, 16)
                    stores += 1
            sp.wait_ge(out_done, 16 * stores)

        @block.gpsimd
        def _(pool):
            nc.gpsimd.memset(w_qkv[:, :, :], 0.0)
            nc.gpsimd.memset(w_gat[0][:, :, :], 0.0)
            nc.gpsimd.memset(w_gat[1][:, :, :], 0.0)
            nc.gpsimd.memset(no_edge[:, :, 0:1], 0)
            nc.gpsimd.memset(no_edge[:, :, 1:2], NO_NODE)
            pool.drain()
            nc.gpsimd.memset(ones[:, :], 1.0)
            nc.gpsimd.iota(iota[:, :], [[1, P]], base=0, channel_multiplier=0,
                           allow_small_or_imprecise_dtypes=True)
            nc.gpsimd.iota(col_no[:, :], [[0, P]], base=0, channel_multiplier=1,
                           allow_small_or_imprecise_dtypes=True)
            nc.gpsimd.iota(chunk_no, [[1, NC_]], base=0, channel_multiplier=0,
                           allow_small_or_imprecise_dtypes=True)
            nc.gpsimd.iota(iota_bf[:, :], [[1, P]], base=0, channel_multiplier=0,
                           allow_small_or_imprecise_dtypes=True)
            nc.gpsimd.memset(ones_bf[:, :], 1.0)
            pool.drain()
            nc.gpsimd.memset(cumul[:, :], 0.0).then_inc(iotas, 1)

            pool.wait_ge(keys_split, 2)
            for block_of, node, pair, key in ((dst_block, dst32, src_pairs, src32),
                                              (src_block, src32, dst_pairs, dst32)):
                nc.gpsimd.tensor_scalar(running[0], block_of, -float(P * NB - 1), None, ALU.mult)
                nc.gpsimd.tensor_scalar(sorted_at, node, float(NB), None, ALU.mult)
                nc.gpsimd.tensor_copy(pair[:, :, 1], key)
                pool.drain()
                nc.gpsimd.tensor_tensor(sorted_at, sorted_at, running[0], ALU.add)
                pool.drain()
                nc.gpsimd.tensor_copy(pair[:, :, 0], sorted_at)
                pool.drain()
            pool.sem_inc(pairs_made, 1)

            def scatter(i, own, first=False, late=False):
                for part in range(2):
                    n = SCH[part]
                    if n:
                        t0 = i * SC + part * SC0
                        if own:
                            if not first:
                                pool.wait_ge(scattered[part], i * (16 * n))
                                pool.sem_inc(started, 1)
                            nc.gpsimd.tensor_copy(at_stage[part][:, 0:n], sorted_at[:, bass.ds(t0, n)])
                            nc.gpsimd.tensor_copy(pair_stage[part][:, 0:n, :], src_pairs[:, bass.ds(t0, n), :])\
                              .then_inc(staged_pairs, 1)
                        parts = sum(1 for c in SCH if c)
                        if own:
                            by_act = (STAGED_HI - STAGED_LO) * parts if late else 0
                            pool.wait_ge(staged_pairs, i * parts + (part + 1 - by_act))
                        else:
                            pool.wait_ge(staged_by_act, i * parts + (part + 1 - STAGED_LO * parts))
                        pool.sem_inc(started, 1)
                        for u in range(n):
                            nc.gpsimd.indirect_dma_start(
                                by_src,
                                bass.IndirectOffsetOnAxis(ap=at_stage[part][:, u:u + 1].bitcast(u32), axis=0),
                                pair_stage[part][:, u, :], None).then_inc(scattered[part], 16)

            pool.wait_ge(places_ready, 1)
            scatter(0, True, first=True)
            if STAGED_LO > 1:
                with pool.Fori(1, STAGED_LO) as i:
                    scatter(i, True)
            if STAGED_LO < STAGED_HI:
                with pool.Fori(STAGED_LO, STAGED_HI) as i:
                    scatter(i, False)
            if STAGED_HI < units:
                pool.wait_ge(places_ready, len(SEGMENTS))
                with pool.Fori(STAGED_HI, units) as i:
                    scatter(i, True, late=True)

            for p in range(6):
                pool.wait_ge(table_out[p], 16 * NH)
                with pool.Fori(0, ITERS) as it:
                    for s in range(S):
                        pool.wait_ge(staged[p], it * S + s + 1)
                        pool.sem_inc(started, 1)
                        for t in range(T):
                            nc.gpsimd.indirect_dma_start(
                                (rows_e if p >= 4 else rows)[s][:, t, 0:WIDTH[p]], None, TABLE[p],
                                bass.IndirectOffsetOnAxis(ap=index[s][:, t:t + 1].bitcast(u32), axis=0))\
                              .then_inc(landed[p][s], 16)

        @block.scalar
        def _(act):
            act.wait_ge(consts, 1)
            nc.scalar.activation(mean[:, 0:1], half_up[:, 0:1], ACT.Sign)
            act.wait_ge(keys_split, 2)
            for block_of, to, lo, hi in ((src_block, cumul_src, COUNTED_BY_DVE - 1, NBLK - 1), (dst_block, cumul, 0, NBLK)):
                with act.Fori(lo, hi) as b:
                    act.drain()
                    nc.scalar.activation(sign_out, block_of, ACT.Sign, bias=half_up[:, bass.ds(b, 1)],
                                         scale=-1.0, accum_out=to[:, bass.ds(b + 1, 1)])
                act.drain()
                nc.scalar.activation(mean[:, 0:1], ones[:, 0:1], ACT.Copy).then_inc(act_counted, 1)

            for g, (lo, hi) in enumerate(SEGMENTS):
                hi = min(hi, STAGED_HI)
                if g and lo < hi:
                    act.wait_ge(places_ready, g + 1)
                    with act.Fori(lo, hi) as i:
                        for part in range(2):
                            n = SCH[part]
                            if n:
                                t0 = i * SC + part * SC0
                                act.wait_ge(scattered[part], i * (16 * n))
                                act.sem_inc(started, 1)
                                nc.scalar.activation(at_stage[part][:, 0:n], sorted_at[:, bass.ds(t0, n)], ACT.Copy)
                                nc.scalar.activation(pair_stage[part][:, 0:n, :], src_pairs[:, bass.ds(t0, n), :],
                                                     ACT.Copy).then_inc(staged_by_act, 1)

            def turn_h(i, h):
                for half, (lo, hi) in enumerate(HALVES):
                    act.wait_ge(h_ready[i], half + 1)
                    with act.Fori(lo, hi) as j:
                        nc.scalar.activation(h_stage.rearrange("p (b f) -> p b f", f=F),
                                             h[:, bass.ds(j * (2 * PROJ), 2 * PROJ), :], ACT.Copy)\
                          .then_inc(h_staged[i], 1)
                        act.wait_ge(h_turned[i], j + 1)
                        nc.scalar.activation(h_t, banks(0, 2)[:, 0:PROJ * P], ACT.Copy)\
                          .then_inc(h_t_ready[i], 1)

            roots = [0]
            norms = [0]

            def root(of=slice(0, NB)):
                roots[0] += 1
                act.wait_ge(root_in, roots[0])
                nc.scalar.activation(rstd[:, of], rstd[:, of], ACT.Sqrt).then_inc(root_out, 1)

            def norm():
                for h in range(NH):
                    act.wait_ge(centered_ready, norms[0] * NH + h + 1)
                    nc.scalar.activation(squares[:, HB[h], :], centered[:, HB[h], :], ACT.Square)\
                      .then_inc(squared, 1)
                    root(HB[h])
                norms[0] += 1

            root()
            norm()
            norm()
            turn_h(0, acc64)
            p = 2
            for n in range(2):
                act.wait_ge(turned[p], n + 1)
                nc.scalar.activation(onehot_t, turned_hot, ACT.Copy).then_inc(turned_read[p], 1)
            with act.Fori(0, ITERS) as it:
                for s in range(S):
                    act.wait_ge(exp_in[p], it * S + s + 1)
                    nc.scalar.activation(rows[s][:, :, KV:KV + HEADS],
                                         att[:, :].rearrange("p (t h) -> p t h", h=HEADS), ACT.Exp)\
                      .then_inc(exp_out[p], 1)
                    act.wait_ge(turned[p], it * S + s + 3)
                    nc.scalar.activation(onehot_t, turned_hot, ACT.Copy).then_inc(turned_read[p], 1)

            root()
            norm()
            norm()
            for i in range(2):
                turn_h(1 + i, aux)
                p = 4 + i

                def score(n, s, it):
                    act.wait_ge(hot_ready[p], n + 1)
                    act.wait_ge(landed[p][s], it * (16 * T) + 16 * T)
                    for t in range(T):
                        last = nc.scalar.activation(scores[:, t, :], nothot[s % 2][:, t, :], ACT.Identity,
                                                    bias=rows_e[s][:, t, F:F + 1], scale=-BIG)
                    last.then_inc(scores_ready[p], 1)

                def invert(s):
                    nc.scalar.activation(hot_e[s % 2], nothot[s % 2], ACT.Copy, bias=1.0, scale=-1.0)\
                      .then_inc(turned_read[p], 1)

                def attend(n, s, it, first, more):
                    if more:
                        act.wait_ge(turned[p], n + 1)
                        score(n + 1, (s + 1) % S, it + (s + 1) // S)
                        if not first:
                            act.wait_ge(used[p], n)
                        invert((s + 1) % S)
                    act.wait_ge(nodes_ready[p], n + 1)
                    nc.scalar.activation(fade[s % 2][:, :], fade_in[:, :], ACT.Exp).then_inc(fade_out[p], 1)
                    act.wait_ge(exp_in[p], n + 1)
                    nc.scalar.activation(weight[:, :], edge_b[:, :], ACT.Exp).then_inc(exp_out[p], 1)

                score(0, 0, 0)
                invert(0)
                for s in range(S):
                    attend(s, s, 0, s == 0, True)
                if ITERS > 2:
                    with act.Fori(1, ITERS - 1) as it:
                        for s in range(S):
                            attend(it * S + s, s, it, False, True)
                for s in range(S):
                    attend((ITERS - 1) * S + s, s, ITERS - 1, False, s < S - 1)

        @block.tensor
        def _(pe):
            mm = nc.tensor.matmul
            for step, d in enumerate((1, 0)):
                pe.wait_ge(counted, step + 1)
                mm(psum[:, d, 0:P], ones[:, :], counts[d][:, :], start=True, stop=True)
                mm(psum[:, d, P:2 * P], before[:, :], counts[d][:, :], start=True, stop=True)
                mm(psum[:, d, 2 * P:2 * P + 1], counts[d][:, :], ones[:, 0:1], start=True, stop=True)\
                    .then_inc(totals, 1)
                pe.wait_ge(columns, step + 1)
                mm(psum[:, d, 2 * P + 1:2 * P + 2], upto[:, :], col[1][:, :], start=True, stop=True)\
                    .then_inc(cum_cols, 1)
                pe.wait_ge(began_ready, step + 1)
                for j, c in enumerate(range(0, NC_, 512)):
                    w = min(512, NC_ - c)
                    if j or step:
                        pe.wait_ge(tables_read, step * len(range(0, NC_, 512)) + j)
                    mm(psum[:, 2, 0:w], real128[:, :], began[:, c:c + w], start=True, stop=True)
                    mm(psum[:, 3, 0:w], delta_wide[:, :], began[:, c:c + w], start=True, stop=True)\
                        .then_inc(tables_psum, 1)
            with pe.Fori(0, NBAT // 2) as n:
                for q in range(2):
                    pe.wait_ge(deg_hot, n * 2 + q + 1)
                    for k in range(CB):
                        for g in range(G):
                            last = mm(psum[:, 4 + q, k:k + 1], hot_bf[q][:, k * G + g, :], ones_bf[:, :],
                                      start=(g == 0), stop=(g == G - 1))
                    last.then_inc(deg_psum, 1)

            def linear(p):
                with pe.Fori(0, ITERS) as it:
                    for s in range(S):
                        q = s % 2
                        pe.wait_ge(hot_ready[p], it * S + s + 1)
                        pe.wait_ge(landed[p][s], it * (16 * T) + 16 * T)
                        pe.wait_ge(added[p][q], it * (CB * S // 2) + CB * (s // 2) + 1)
                        for k in range(CB):
                            for g in range(G):
                                last = mm(psum[:, 2 * q + k // 4, (k % 4) * F:(k % 4) * F + F], onehot[q][:, k * G + g, :],
                                          rows[s][:, k * G + g, 0:F], start=(g == 0), stop=(g == G - 1))
                            if k == CB // 2 - 1:
                                last.then_inc(summed[p], 1)
                            if k == CB - 1:
                                last.then_inc(used[p], 1)

            def project(i, w, width):
                with pe.Fori(0, NB // (2 * PROJ)) as j:
                    for k in range(PROJ):
                        if k == 0:
                            pe.wait_ge(h_staged[i], j + 1)
                        last = nc.tensor.transpose(banks(0, 2)[:, k * P:k * P + P],
                                                   h_stage[:, k * P:k * P + P], ident[:, :])
                    last.then_inc(h_turned[i], 1)
                    pe.wait_ge(h_t_ready[i], j + 1)
                    pe.wait_ge(proj_read[i], j * PROJ + 1)
                    for k in range(PROJ):
                        mm(psum[:, 2 + k, 0:width], h_t[:, k * P:k * P + P], w, start=True, stop=True)\
                            .then_inc(projected[i], 1)

            linear(0)
            linear(1)

            pe.wait_ge(weights_in, 16 * 17)
            project(0, w_qkv[:, :, :].rearrange("p a b -> p (a b)"), 6 * F)
            p = 2

            def turn(buf):
                for t in range(T):
                    last = nc.tensor.transpose(turned_hot[:, t, :], buf[:, t, :], ident_bf[:, :])
                last.then_inc(turned[p], 1)

            def edge_nodes(n):
                _, blocks = nc.values_load_multi_w_load_instructions(
                    chunk_int[BLOCK_ROW[1]:BLOCK_ROW[1] + 1, bass.ds(n * CB, CB)],
                    engines=PE_ONLY, min_val=0, max_val=NBLK,
                    skip_runtime_bounds_check_because="a count of blocks")
                pe.wait_ge(turned_read[p], n + 1)
                pe.wait_ge(spread[p], n + 1)
                for t in range(T):
                    last = mm(psum[:, 4 + t // 8, (t % 8) * F:(t % 8) * F + F], onehot_t[:, t, :],
                              aux[:, bass.ds(blocks[t // G], 1), :].rearrange("p o f -> p (o f)"),
                              start=True, stop=True)
                last.then_inc(nodes_ready[p], 1)

            pe.wait_ge(hot_ready[p], 1)
            pe.wait_ge(proj_read[0], PROJ * (NB // (2 * PROJ)) + 1)
            turn(onehot_bf[0])
            edge_nodes(0)
            pe.wait_ge(hot_ready[p], 2)
            turn(onehot_bf[1])
            with pe.Fori(0, ITERS) as it:
                for s in range(S):
                    n = it * S + s
                    edge_nodes(n + 1)
                    pe.wait_ge(hot_ready[p], n + 3)
                    turn(onehot_bf[(s + 2) % 4])
                    pe.wait_ge(rows_ready[p], n + 1)
                    pe.wait_ge(added[p][0], n * CB + 1)
                    parts = (upper(rows[s][:, :, F:ROW]), upper(rest), last_part)
                    for k in range(CB):
                        for g in range(G):
                            for i, part in enumerate(parts):
                                last = mm(psum[:, 6 + k // 4, (k % 4) * MSG:(k % 4) * MSG + MSG],
                                          onehot_bf[s][:, k * G + g, :], part[:, k * G + g, :],
                                          start=(g == 0 and i == 0), stop=(g == G - 1 and i == 2))
                        if k == CB // 2 - 1:
                            last.then_inc(summed[p], 1)
                        if k == CB - 1:
                            last.then_inc(used[p], 1)

            linear(3)

            for i in range(2):
                p = 4 + i
                project(1 + i, w_gat[i][:, :, :].rearrange("p a b -> p (a b)"), 2 * (F + 2))
                pe.wait_ge(tabs_ready[i], 1)
                nc.tensor.transpose(psum[:, 0, 0:P], ad_tab[:, :], ident[:, :])
                nc.tensor.transpose(psum[:, 0, P:2 * P], self_tab[:, :], ident[:, :]).then_inc(tabs_turned[i], 1)
                pe.wait_ge(tabs_t_ready[i], 1)
                pieces = list(range(0, NC_, 512))
                assert len(pieces) <= 4
                for side in range(2):
                    for j, c in enumerate(pieces):
                        w = min(512, NC_ - c)
                        last = mm(psum[:, side * 4 + j, 0:w], tab_t[:, side, :], block_hot[:, c:c + w],
                                  start=True, stop=True)
                last.then_inc(spread_psum[i], 1)

                def turn_scores(n):
                    pe.wait_ge(scores_ready[p], n + 1)
                    for t in range(T):
                        last = nc.tensor.transpose(banks(0, 4)[:, t * P:t * P + P], scores[:, t, :], ident[:, :])
                    last.then_inc(turned[p], 1)

                def attend(n, s, more):
                    pe.wait_ge(nodes_ready[p], n + 1)
                    for t in range(T):
                        for i in range(3):
                            last = mm(psum[:, 4, 2 * t:2 * t + 2], hot_te[:, t, :],
                                      upper(node_pair[i][:, :, :])[:, t // G, :], start=(i == 0), stop=(i == 2))
                    last.then_inc(spread[p], 1)
                    if more:
                        turn_scores(n + 1)
                    pe.wait_ge(turned_read[p], n + 1)
                    pe.wait_ge(rows_ready[p], n + 1)
                    for k in range(CB):
                        for g in range(G):
                            last = mm(psum[:, 5 + k // 4, (k % 4) * 65:(k % 4) * 65 + 65],
                                      hot_e[s % 2][:, k * G + g, :], rows_e[s][:, k * G + g, :],
                                      start=(g == 0), stop=(g == G - 1))
                        if k == CB // 2 - 1:
                            last.then_inc(summed[p], 1)
                        if k == CB - 1:
                            last.then_inc(used[p], 1)

                turn_scores(0)
                if ITERS > 1:
                    with pe.Fori(0, ITERS - 1) as it:
                        for s in range(S):
                            attend(it * S + s, s, True)
                for s in range(S):
                    attend((ITERS - 1) * S + s, s, s < S - 1)

        @block.vector
        def _(dve):
            v = nc.vector

            def wide(a, shape):
                return a.to_broadcast(shape)

            dve.wait_ge(iotas, 1)
            v.tensor_tensor(ident[:, :], iota[:, :], col_no[:, :], ALU.is_equal)
            v.tensor_tensor(ident_bf[:, :], iota[:, :], col_no[:, :], ALU.is_equal)
            v.tensor_tensor(before[:, :], iota[:, :], col_no[:, :], ALU.is_gt)
            v.tensor_tensor(upto[:, :], iota[:, :], col_no[:, :], ALU.is_ge)
            v.tensor_scalar(real128[:, :], col_no[:, :], float(NBLK), float(P), ALU.is_lt, ALU.mult)
            v.tensor_scalar(half_up[:, :], iota[:, :], 0.5, None, ALU.add)
            dve.drain().then_inc(consts, 1)

            dve.wait_ge(edges_in, 32)
            v.tensor_scalar(block_int, dst32, 7, None, ALU.logical_shift_right)
            dve.drain()
            v.tensor_copy(dst_block, block_int).then_inc(keys_split, 1)
            dve.drain()
            v.tensor_scalar(block_int, src32, 7, None, ALU.logical_shift_right)
            v.memset(counts[0][:, :], 0.0)
            v.memset(counts[1][:, :], 0.0)
            dve.drain()
            v.tensor_copy(src_block, block_int)
            dve.drain().then_inc(keys_split, 1)
            v.memset(cumul_src[:, NBLK:NBLK + 1], float(EP))
            with dve.Fori(0, COUNTED_BY_DVE) as b:
                dve.drain()
                v.tensor_scalar(block_hit_bf, src_block, iota[:, bass.ds(b, 1)], 0.0, ALU.is_equal, ALU.add,
                                accum_out=counts[1][:, bass.ds(b, 1)])
            dve.drain()
            def chunk_tables(step, d):
                v.tensor_copy(col[0][:, :], psum[:, d, 2 * P:2 * P + 1])
                v.tensor_scalar(col_int[:, :], psum[:, d, 2 * P:2 * P + 1], float(CH - 1), None, ALU.add)
                dve.drain()
                v.tensor_scalar(col_int[:, :], col_int[:, :], CH.bit_length() - 1, None, ALU.logical_shift_right)
                dve.drain()
                v.tensor_copy(col[1][:, :], col_int[:, :])
                dve.drain()
                v.scalar_tensor_tensor(col[2][:, :], col[1][:, :], float(-CH), col[0][:, :], ALU.mult, ALU.add)\
                    .then_inc(columns, 1)
                dve.drain()
                if step:
                    dve.wait_ge(tables_psum, len(range(0, NC_, 512)))
                v.tensor_copy(delta_wide[:, :], wide(col[2][:, 0:1], [P, P]))
                dve.wait_ge(cum_cols, step + 1)
                v.tensor_copy(col[3][:, :], psum[:, d, 2 * P + 1:2 * P + 2])
                dve.drain()
                v.tensor_scalar(began, chunk_no, col[3][:, 0:1], None, ALU.is_ge)
                dve.drain()
                v.tensor_copy(small[3][:, 0:1], col[3][:, :]).then_inc(began_ready, 1)
                for j, c in enumerate(range(0, NC_, 512)):
                    w = min(512, NC_ - c)
                    dve.wait_ge(tables_psum, step * len(range(0, NC_, 512)) + j + 1)
                    v.tensor_copy(block128[d][:, c:c + w], psum[:, 2, 0:w])
                    r = BLOCK_ROW[d]
                    v.tensor_scalar(chunk_int[r:r + 1, c:c + w], psum[r:r + 1, 2, 0:w], 1.0 / P, None, ALU.mult)
                    r = OFFSET_ROW[d]
                    dve.drain()
                    v.scalar_tensor_tensor(running[0][r:r + 1, c:c + w], chunk_no[r:r + 1, c:c + w], float(CH),
                                           psum[r:r + 1, 3, 0:w], ALU.mult, ALU.add).then_inc(tables_read, 1)
                    dve.drain()
                    v.tensor_scalar(chunk_int[r:r + 1, c:c + w], running[0][r:r + 1, c:c + w], float(E), None, ALU.min)
                dve.drain().then_inc(offsets_ready, 1)

            dve.wait_ge(act_counted, 1)
            v.tensor_scalar(cumul_src[:, COUNTED_BY_DVE:NBLK], cumul_src[:, COUNTED_BY_DVE:NBLK], float(EP), 0.5, ALU.add, ALU.mult)
            dve.drain()
            v.tensor_tensor(counts[1][:, COUNTED_BY_DVE:NBLK], cumul_src[:, COUNTED_BY_DVE + 1:NBLK + 1], cumul_src[:, COUNTED_BY_DVE:NBLK],
                            ALU.subtract)
            dve.drain().then_inc(counted, 1)
            v.memset(small[0][:, :], 0.0)
            dve.wait_ge(totals, 1)
            v.tensor_copy(small[2][:, :], psum[:, 1, 0:P])
            dve.drain()
            v.tensor_tensor_scan(small[1][:, :], small[2][:, :], small[0][:, :], 0.0, ALU.add, ALU.add)
            dve.drain()
            v.scalar_tensor_tensor(small[1][:, :], small[1][:, :], -1.0, small[2][:, :], ALU.add, ALU.subtract)
            dve.drain()
            v.tensor_tensor(small[1][:, :], small[1][:, :], psum[:, 1, P:2 * P], ALU.add)
            dve.drain()
            def find_places(g, lo, hi):
                part = slice(lo * SC, hi * SC)
                n = (hi - lo) * SC
                with dve.Fori(0, -(-NBLK // 2)) as b2:
                    for i in range(2):
                        v.tensor_scalar(block_hit[i][:, 0:n], src_block[:, part], iota[:, bass.ds(b2 * 2 + i, 1)],
                                        None, ALU.is_equal)
                    dve.drain()
                    for i in range(2):
                        v.tensor_tensor_scan(running[i][:, part], block_hit[i][:, 0:n], block_hit[i][:, 0:n],
                                             small[1][:, bass.ds(b2 * 2 + i, 1)], ALU.add, ALU.bypass)
                    dve.drain()
                    for i in range(2):
                        v.tensor_scalar(small[1][:, bass.ds(b2 * 2 + i, 1)], running[i][:, hi * SC - 1:hi * SC],
                                        1.0, None, ALU.mult)
                    v.copy_predicated(sorted_at[:, part], block_hit[0][:, 0:n].bitcast(i32), running[0][:, part])
                    dve.drain()
                    v.copy_predicated(sorted_at[:, part], block_hit[1][:, 0:n].bitcast(i32), running[1][:, part])
                    dve.drain()
                if hi == EP // SC:
                    v.memset(xr[:, :], 0.0).then_inc(x_region_free, 1)
                dve.drain().then_inc(places_ready, 1)

            dve.wait_ge(pairs_made, 1)
            dve.wait_ge(pairs_out, 48)
            for g in range(len(SEGMENTS) - 1):
                find_places(g, *SEGMENTS[g])
            chunk_tables(0, 1)
            dve.wait_ge(act_counted, 2)
            v.tensor_scalar(cumul[:, 1:NBLK + 1], cumul[:, 1:NBLK + 1], float(EP), 0.5, ALU.add, ALU.mult)
            dve.drain()
            v.tensor_tensor(counts[0][:, 0:NBLK], cumul[:, 1:NBLK + 1], cumul[:, 0:NBLK], ALU.subtract)
            dve.drain().then_inc(counted, 1)
            dve.wait_ge(totals, 2)
            chunk_tables(1, 0)
            find_places(len(SEGMENTS) - 1, *SEGMENTS[-1])

            for ahead in [a for p in LINEAR for a in added[p]] + [added[2][0], spread[2], *proj_read]:
                dve.sem_inc(ahead, 1)

            def load_blocks(direction, n):
                _, blocks = nc.values_load_multi_w_load_instructions(
                    chunk_int[BLOCK_ROW[direction]:BLOCK_ROW[direction] + 1, bass.ds(n * CB, CB)],
                    engines=DVE_ONLY, min_val=0, max_val=NBLK,
                    skip_runtime_bounds_check_because="a count of blocks")
                return blocks

            def keys_to_local(direction, n, drained=True):
                if drained:
                    dve.drain()
                v.tensor_tensor(local[:, :].rearrange("p (k g) -> p k g", g=G),
                                pairs[direction][:, bass.ds(n * CB, CB), :, 1],
                                wide(block128[direction][:, bass.ds(n * CB, CB)].unsqueeze(2), [P, CB, G]),
                                ALU.subtract)

            def compare(to, op):
                return v.tensor_tensor(to, wide(iota_bf[:, :].unsqueeze(1), [P, T, P]),
                                       wide(local[:, :].unsqueeze(2), [P, T, P]), op)

            def stage_index(p, s, n):
                v.tensor_scalar(index[s][:, :].rearrange("p (k g) -> p k g", g=G),
                                pairs[DIRECTION[p]][:, bass.ds(n * CB, CB), :, 0], 0, None, ALU.add)\
                    .then_inc(staged[p], 1)

            deg = dis_dst
            v.memset(deg[:, :], 0.0)

            def add_deg(n, q):
                blocks = load_blocks(0, n)
                for k in range(CB):
                    dve.drain()
                    if k == 0:
                        dve.wait_ge(deg_psum, n + 1)
                    v.tensor_tensor(deg[:, bass.ds(blocks[k], 1)], deg[:, bass.ds(blocks[k], 1)],
                                    psum[:, 4 + q, k:k + 1], ALU.add)

            def deg_hots(n, q):
                dve.drain()
                dve.wait_ge(loaded[0], n + 1)
                keys_to_local(0, n, False)
                dve.drain()
                compare(hot_bf[q], ALU.is_equal).then_inc(deg_hot, 1)

            dve.wait_ge(pairs_out, 48)
            deg_hots(0, 0)
            with dve.Fori(0, NBAT // 2) as i:
                for q in range(2):
                    if q == 0:
                        deg_hots(i * 2 + 1, 1)
                    add_deg(i * 2 + q, q)
                    if q == 1:
                        deg_hots(i * 2 + 2, 0)
            dve.drain()

            roots = [0]

            def reciprocal_root(of=slice(0, NB)):
                roots[0] += 1
                dve.drain().then_inc(root_in, 1)
                dve.wait_ge(root_out, roots[0])
                v.reciprocal(rstd[:, of], rstd[:, of])
                dve.drain()

            def inverse_root(t):
                v.tensor_scalar(mean[:, :], t[:, :], 0.0, None, ALU.is_gt)
                v.tensor_scalar(rstd[:, :], t[:, :], 1.0, None, ALU.max)
                dve.drain()
                reciprocal_root()
                v.tensor_tensor(t[:, :], mean[:, :], rstd[:, :], ALU.mult)
                dve.drain()

            norms = [0]

            def norm_relu(to, per_node=None, done=None):
                def wide_half(a, of):
                    return wide(a[:, of].unsqueeze(2), [P, of.stop - of.start, F])

                def means(h):
                    of = HB[h]
                    v.tensor_reduce(mean[:, of], x[:, of, :], AX.X, ALU.add)
                    dve.drain()
                    v.tensor_scalar(mean[:, of], mean[:, of], 1.0 / F, None, ALU.mult)
                    dve.drain()

                def center(h):
                    of = HB[h]
                    v.tensor_tensor(centered[:, of, :], x[:, of, :], wide_half(mean, of), ALU.subtract)
                    dve.drain().then_inc(centered_ready, 1)

                def variances(h):
                    of = HB[h]
                    dve.wait_ge(squared, norms[0] * NH + h + 1)
                    v.tensor_reduce(rstd[:, of], squares[:, of, :], AX.X, ALU.add)
                    dve.drain()
                    v.tensor_scalar(rstd[:, of], rstd[:, of], 1.0 / F, 1e-5, ALU.mult, ALU.add)
                    roots[0] += 1
                    dve.drain().then_inc(root_in, 1)
                    return roots[0]

                def finish(h, root):
                    of = HB[h]
                    dve.wait_ge(root_out, root)
                    v.reciprocal(rstd[:, of], rstd[:, of])
                    dve.drain()
                    if per_node is not None:
                        v.tensor_tensor(rstd[:, of], rstd[:, of], per_node[:, of], ALU.mult)
                        dve.drain()
                    v.scalar_tensor_tensor(to[:, of, :], centered[:, of, :], 0.0, wide_half(rstd, of),
                                           ALU.max, ALU.mult)
                    if done is not None:
                        dve.drain().then_inc(done, 1)
                    else:
                        dve.drain()

                means(0)
                center(0)
                if NH > 1:
                    means(1)
                first = variances(0)
                if NH > 1:
                    center(1)
                finish(0, first)
                if NH > 1:
                    finish(1, variances(1))
                norms[0] += 1

            def scaled(to, a, per_node):
                return v.tensor_tensor(to, a, wide(per_node.unsqueeze(2), [P, NB, F]), ALU.mult)

            def add_to_x(scalar, a):
                v.scalar_tensor_tensor(x, a, scalar, x, ALU.mult, ALU.add)

            def all_pairs_in(p):
                dve.wait_ge(loaded[DIRECTION[p]], NBAT + S)

            def first_indices(p):
                all_pairs_in(p)
                for s in range(S):
                    stage_index(p, s, s)

            def linear(p):
                d = DIRECTION[p]
                first_indices(p)
                keys_to_local(d, 0)
                dve.wait_ge(table_out[p], 16 * NH)
                dve.drain()
                compare(onehot[0], ALU.is_equal).then_inc(hot_ready[p], 1)
                with dve.Fori(0, ITERS) as it:
                    for s in range(S):
                        q = s % 2
                        n = it * S + s
                        dve.drain()
                        keys_to_local(d, n + 1)
                        dve.drain()
                        compare(onehot[1 - q], ALU.is_equal).then_inc(hot_ready[p], 1)
                        blocks = load_blocks(d, n)
                        for k in range(CB):
                            dve.drain()
                            if k == 0:
                                dve.wait_ge(summed[p], n + 1)
                            if k == CB // 2:
                                dve.wait_ge(used[p], n + 1)
                            v.tensor_tensor(acc64[:, bass.ds(blocks[k], 1), :].rearrange("p o f -> p (o f)"),
                                            acc64[:, bass.ds(blocks[k], 1), :].rearrange("p o f -> p (o f)"),
                                            psum[:, 2 * q + k // 4, (k % 4) * F:(k % 4) * F + F], ALU.add).then_inc(added[p][q], 1)
                        stage_index(p, s, n + S)
                dve.drain()

            dve.wait_ge(weights_in, 16 * 17)
            w_times = small[0][:, 0:2 * F].rearrange("p (a b) -> p a b", b=F)
            for w, a_src, a_dst in ((w_gat[0], vecs[0], vecs[1]), (w_gat[1], vecs[3], vecs[4])):
                for c, a in ((F, a_src), (F + 1, a_dst)):
                    v.tensor_tensor(w_times, w[:, :, 0:F], wide(a[:, :].unsqueeze(1), [P, 2, F]), ALU.mult)
                    dve.drain()
                    v.tensor_reduce(w[:, :, c], w_times, AX.X, ALU.add)
                    dve.drain()

            inverse_root(dis_dst)
            dve.wait_ge(x_in_sem, 32 if TAIL else 16)
            norm_relu(acc64)
            scaled(y_stage, acc64, dis_dst[:, :]).then_inc(table_ready[0], NH)
            add_to_x(alpha[:, 0:1], acc64)
            v.tensor_tensor(mean[:, :], dis_dst[:, :], dis_dst[:, :], ALU.mult)
            dve.drain()
            v.memset(accr[:, :], 0.0)
            linear(0)
            for h in range(NH):
                v.tensor_tensor(y_stage[:, HB[h], :], acc64[:, HB[h], :],
                                wide(mean[:, HB[h]].unsqueeze(2), [P, HB[h].stop - HB[h].start, F]), ALU.mult)\
                    .then_inc(table_ready[1], 1)
            dve.drain()
            scaled(acc64, acc64, dis_dst[:, :])
            dve.drain()
            add_to_x(alpha[:, 1:2], acc64)
            dve.drain()
            v.memset(accr[:, :], 0.0)
            linear(1)
            scaled(acc64, acc64, dis_dst[:, :])
            dve.drain()
            add_to_x(alpha[:, 2:3], acc64)
            dve.drain()

            norm_relu(acc64, done=h_ready[0])
            for lo, hi in HALVES:
                with dve.Fori(lo, hi) as j:
                    for k in range(PROJ):
                        b2 = j * (2 * PROJ) + 2 * k
                        o = psum[:, 2 + k, 0:6 * F].rearrange("p (b f) -> p b f", b=2)
                        dve.wait_ge(projected[0], j * PROJ + k + 1)
                        v.tensor_scalar(aux[:, bass.ds(b2, 2), :], o[:, :, 0:F], 1.0, None, ALU.mult)
                        v.tensor_scalar(kv_stage[:, bass.ds(b2, 2), :], o[:, :, F:3 * F], 1.0, None, ALU.mult)\
                            .then_inc(proj_read[0], 1)
                dve.drain().then_inc(table_ready[2], 1)
            v.memset(accr[:, :], 0.0)
            first_indices(2)
            dve.wait_ge(table_out[2], 16 * NH)
            p = 2
            for s in range(S):
                v.memset(rows[s][:, :, ROW - 1:ROW], 1.0)
            for n in range(2):
                keys_to_local(1, n)
                dve.drain()
                compare(onehot_bf[n], ALU.is_equal).then_inc(hot_ready[p], 1)

            def add_attention(n):
                blocks = load_blocks(1, n)
                for k in range(CB):
                    dve.drain()
                    if k == 0:
                        dve.wait_ge(summed[p], n + 1)
                    if k == CB // 2:
                        dve.wait_ge(used[p], n + 1)
                    a = acc69[:, bass.ds(blocks[k], 1), :].rearrange("p o f -> p (o f)")
                    v.tensor_tensor(a, a, psum[:, 6 + k // 4, (k % 4) * MSG:(k % 4) * MSG + MSG], ALU.add)\
                        .then_inc(added[p][0], 1)

            def attend_q(n, s, it, first):
                dve.drain()
                dve.wait_ge(landed[p][s], it * (16 * T) + 16 * T)
                dve.wait_ge(nodes_ready[p], n + 1)
                products = rows[s][:, :, 0:F]
                v.tensor_tensor(products, products,
                                banks(4, 2).rearrange("p (t f) -> p t f", f=F), ALU.mult)\
                    .then_inc(spread[p], 1)
                dve.drain()
                v.tensor_reduce(att[:, :].rearrange("p (t h) -> p t h", h=HEADS),
                                products.rearrange("p t (h d) -> p t h d", d=DH), AX.X, ALU.add)
                dve.drain()
                v.tensor_scalar(att[:, :], att[:, :], -10.0, 10.0, ALU.max, ALU.min).then_inc(exp_in[p], 1)
                keys_to_local(1, n + 2)
                dve.drain()
                compare(onehot_bf[(s + 2) % 4], ALU.is_equal).then_inc(hot_ready[p], 1)
                if not first:
                    add_attention(n - 1)
                    stage_index(p, (s - 1) % S, n - 1 + S)
                dve.wait_ge(exp_out[p], n + 1)
                vv = rows[s][:, :, F:KV].rearrange("p t (h d) -> p t h d", d=DH)
                v.tensor_tensor(vv, vv, wide(rows[s][:, :, KV:KV + HEADS].unsqueeze(3), [P, T, HEADS, DH]),
                                ALU.mult)
                dve.drain()
                msg = rows[s][:, :, F:ROW]
                v.tensor_tensor(rest, msg, upper(msg), ALU.subtract)
                dve.drain()
                v.tensor_tensor(last_part, rest, upper(rest), ALU.subtract).then_inc(rows_ready[p], 1)

            for s in range(S):
                attend_q(s, s, 0, s == 0)
            if ITERS > 1:
                with dve.Fori(1, ITERS) as it:
                    for s in range(S):
                        attend_q(it * S + s, s, it, False)
            add_attention(NBAT - 1)
            dve.drain()

            v.tensor_copy(dis_src[:, :], acc69[:, :, F + HEADS])
            den = acc69[:, :, F:F + HEADS]
            v.tensor_scalar(den, den, 1e-8, None, ALU.add)
            dve.drain()
            v.reciprocal(den, den)
            dve.drain()
            num = acc69[:, :, 0:F].rearrange("p b (h d) -> p b h d", d=DH)
            v.tensor_tensor(num, num, wide(den.unsqueeze(3), [P, NB, HEADS, DH]), ALU.mult)
            dve.drain()
            v.tensor_tensor(x, x, acc69[:, :, 0:F], ALU.add)
            inverse_root(dis_src)

            norm_relu(y_stage, per_node=dis_src, done=table_ready[3])
            v.memset(accr[:, :], 0.0)
            linear(3)
            scaled(acc64, acc64, dis_src[:, :])
            dve.drain()
            v.tensor_tensor(x, x, acc64, ALU.add)
            dve.drain()

            def gat(i):
                p = 4 + i
                v.memset(ad_tab[:, :], 0.0)
                v.memset(self_tab[:, :], 0.0)
                dve.drain()
                for lo, hi in HALVES:
                    with dve.Fori(lo, hi) as j:
                        for k in range(PROJ):
                            b2 = j * (2 * PROJ) + 2 * k
                            o = psum[:, 2 + k, 0:2 * (F + 2)].rearrange("p (b f) -> p b f", b=2)
                            dve.wait_ge(projected[1 + i], j * PROJ + k + 1)
                            v.tensor_scalar(ad_tab[:, bass.ds(b2, 2)], o[:, :, F + 1], 1.0, None, ALU.mult)
                            v.tensor_scalar(g_stage[:, bass.ds(b2, 2), :], o[:, :, 0:F + 1], 1.0, None,
                                            ALU.mult).then_inc(proj_read[1 + i], 1)
                    dve.drain().then_inc(table_ready[p], 1)
                v.tensor_tensor(rstd[:, :], g_stage[:, :, F], ad_tab[:, 0:NB], ALU.add)
                v.tensor_copy(acc65[:, :, 0:F], g_stage[:, :, 0:F])
                v.memset(acc65[:, :, F:F + 1], 1.0)
                dve.drain()
                first_indices(p)
                v.scalar_tensor_tensor(self_tab[:, 0:NB], rstd[:, :], 0.2, rstd[:, :], ALU.mult, ALU.max)
                v.tensor_scalar(block_hot, block128[0][:, :], 1.0 / P, col_no[:, 0:1], ALU.mult, ALU.is_equal)
                v.memset(fresh[:, 0:1], -BIG)
                v.tensor_tensor(fresh[:, 1:NC_], block128[0][:, 1:NC_], block128[0][:, 0:NC_ - 1], ALU.not_equal)
                dve.drain()
                v.tensor_scalar(fresh[:, 1:NC_], fresh[:, 1:NC_], -BIG, None, ALU.mult).then_inc(tabs_ready[i], 1)
                dve.wait_ge(tabs_turned[i], 1)
                v.tensor_copy(tab_t[:, :, :], psum[:, 0, 0:2 * P].rearrange("p (a b) -> p a b", a=2))\
                    .then_inc(tabs_t_ready[i], 1)
                dve.wait_ge(spread_psum[i], 1)
                v.tensor_copy(ad_chunk, banks(0, 4)[:, 0:NC_])
                v.tensor_copy(self_chunk, banks(4, 4)[:, 0:NC_])
                dve.wait_ge(table_out[p], 16 * NH)
                dve.drain()

                v.memset(peak[1][:, :], -BIG)
                for n in range(2):
                    keys_to_local(0, n)
                    dve.drain()
                    compare(nothot[n], ALU.not_equal).then_inc(hot_ready[p], 1)

                def add_chunks(n, q):
                    blocks = load_blocks(0, n)
                    dve.drain()
                    dve.wait_ge(fade_out[p], n + 1)
                    for k in range(CB):
                        if k:
                            dve.drain()
                        if k == 0:
                            dve.wait_ge(summed[p], n + 1)
                        if k == CB // 2:
                            dve.wait_ge(used[p], n + 1)
                        a = acc65[:, bass.ds(blocks[k], 1), :].rearrange("p o f -> p (o f)")
                        v.scalar_tensor_tensor(a, a, fade[q][:, k:k + 1],
                                               psum[:, 5 + k // 4, (k % 4) * 65:(k % 4) * 65 + 65],
                                               ALU.mult, ALU.add)

                def attend(n, s, it, first):
                    q = s % 2
                    dve.wait_ge(turned[p], n + 1)
                    v.tensor_reduce(chunk_max[:, :], banks(0, 4).rearrange("p (k e) -> p k e", k=CB),
                                    AX.X, ALU.max)
                    v.tensor_scalar(hot_te, banks(0, 4).rearrange("p (t e) -> p t e", t=T), -BIG / 2, None,
                                    ALU.is_gt)
                    ad_now = ad_chunk[:, bass.ds(n * CB, CB)]
                    self_now = self_chunk[:, bass.ds(n * CB, CB)]
                    fresh_now = fresh[:, bass.ds(n * CB, CB)]
                    dve.drain()
                    v.tensor_tensor(leak[:, :], chunk_max[:, :], ad_now, ALU.add)
                    v.tensor_scalar(node_pair[0][:, :, 0], ad_now, 1.0, None, ALU.mult)
                    v.tensor_copy(peak[q][:, 0:1], peak[1 - q][:, CB:CB + 1])
                    dve.drain()
                    v.scalar_tensor_tensor(leak[:, :], leak[:, :], 0.2, leak[:, :], ALU.mult, ALU.max)
                    dve.drain()
                    v.tensor_tensor(leak[:, :], leak[:, :], self_now, ALU.max)
                    dve.drain()
                    v.tensor_tensor_scan(peak[q][:, 1:CB + 1], fresh_now, leak[:, :], peak[q][:, 0:1],
                                         ALU.add, ALU.max)
                    dve.drain()
                    v.tensor_copy(node_pair[0][:, :, 1], peak[q][:, 1:CB + 1])
                    v.tensor_tensor(fade_in[:, :], peak[q][:, 0:CB], fresh_now, ALU.add)
                    dve.drain()
                    v.tensor_tensor(node_pair[1][:, :, :], node_pair[0][:, :, :], upper(node_pair[0][:, :, :]),
                                    ALU.subtract)
                    v.tensor_tensor(fade_in[:, :], fade_in[:, :], self_now, ALU.max)
                    dve.drain()
                    v.tensor_tensor(node_pair[2][:, :, :], node_pair[1][:, :, :], upper(node_pair[1][:, :, :]),
                                    ALU.subtract)
                    v.tensor_tensor(fade_in[:, :], fade_in[:, :], peak[q][:, 1:CB + 1], ALU.subtract)
                    dve.drain().then_inc(nodes_ready[p], 1)
                    keys_to_local(0, n + 2, False)
                    dve.drain()
                    dve.wait_ge(turned_read[p], n + 1)
                    compare(nothot[q], ALU.not_equal).then_inc(hot_ready[p], 1)
                    dve.wait_ge(spread[p], n + 1)
                    pair = psum[:, 4, 0:2 * T].rearrange("p (t c) -> p t c", c=2)
                    v.tensor_tensor(edge_a[:, :], rows_e[s][:, :, F], pair[:, :, 0], ALU.add)
                    dve.drain()
                    v.scalar_tensor_tensor(edge_a[:, :], edge_a[:, :], 0.2, edge_a[:, :], ALU.mult, ALU.max)
                    dve.drain()
                    v.tensor_tensor(edge_a[:, :], edge_a[:, :], pair[:, :, 1], ALU.subtract)
                    dve.drain()
                    v.tensor_scalar(edge_b[:, :], edge_a[:, :], 0.0, None, ALU.min).then_inc(exp_in[p], 1)
                    if not first:
                        add_chunks(n - 1, 1 - q)
                        stage_index(p, (s - 1) % S, n - 1 + S)
                    dve.wait_ge(exp_out[p], n + 1)
                    v.tensor_tensor(rows_e[s][:, :, 0:F], rows_e[s][:, :, 0:F],
                                    wide(weight[:, :].unsqueeze(2), [P, T, F]), ALU.mult)
                    v.tensor_copy(rows_e[s][:, :, F], weight[:, :])
                    dve.drain().then_inc(rows_ready[p], 1)

                for s in range(S):
                    attend(s, s, 0, s == 0)
                if ITERS > 2:
                    with dve.Fori(1, ITERS - 1) as it:
                        for s in range(S):
                            attend(it * S + s, s, it, False)
                for s in range(S):
                    attend((ITERS - 1) * S + s, s, ITERS - 1, False)
                add_chunks(NBAT - 1, (S - 1) % 2)
                dve.drain()
                den = acc65[:, :, F]
                v.tensor_scalar(mean[:, :], den, 1e-16, None, ALU.add)
                dve.drain()
                v.reciprocal(mean[:, :], mean[:, :])
                dve.drain()

            def out_of_gat(of):
                v.tensor_tensor(aux[:, of, :], acc65[:, of, 0:F],
                                wide(mean[:, of].unsqueeze(2), [P, of.stop - of.start, F]), ALU.mult)
                dve.drain()

            norm_relu(aux, done=h_ready[1])
            gat(0)
            for of in HB:
                out_of_gat(of)
                v.tensor_tensor(aux[:, of, :], aux[:, of, :],
                                wide(vecs[2][:, :].unsqueeze(1), [P, of.stop - of.start, F]), ALU.add)
                dve.drain()
                v.tensor_scalar(aux[:, of, :], aux[:, of, :], 0.0, None, ALU.max)
                dve.drain().then_inc(h_ready[2], 1)
            gat(1)
            for of in HB:
                out_of_gat(of)
                v.tensor_tensor(aux[:, of, :], aux[:, of, :],
                                wide(vecs[5][:, :].unsqueeze(1), [P, of.stop - of.start, F]), ALU.add)
                dve.drain()
                v.tensor_tensor(x[:, of, :], x[:, of, :], aux[:, of, :], ALU.add).then_inc(out_ready, 1)


_INS = ['x', 'src', 'dst', 'L0_gnn_alpha', 'L1_gnn_Wq', 'L1_gnn_Wk', 'L1_gnn_Wv', 'L3_gnn_W1', 'L3_gnn_a_src1',
        'L3_gnn_a_dst1', 'L3_gnn_b1', 'L3_gnn_W2', 'L3_gnn_a_src2', 'L3_gnn_a_dst2', 'L3_gnn_b2']


def kernel(**inputs):
    import numpy as _np
    import concourse.bacc as _bacc
    from concourse.bass_utils import run_bass_kernel_spmd as _run

    nc = _bacc.Bacc("TRN2", target_bir_lowering=False, num_devices=1)
    arrays, args = {}, []
    for name in _INS:
        a = _np.ascontiguousarray(inputs[name])
        arrays[f"in_{name}_dram"] = a
        args.append(nc.dram_tensor(f"in_{name}_dram", a.shape, mybir.dt.from_np(a.dtype), kind="ExternalInput").ap())
    out = nc.dram_tensor("out_0_dram", arrays["in_x_dram"].shape, f32, kind="ExternalOutput").ap()
    gnn_kernel(nc, *args, out)
    r = _run(nc, [arrays], core_ids=[0])
    return r.results[0]["out_0_dram"]
```
